# Optimizing a Trainium2 kernel written in Bass

```python
import numpy as np
import jax
import jax.numpy as jnp

def _softmax(x, axis=-1):
    return jax.nn.softmax(x, axis=axis)

def _gelu(x):
    return jax.nn.gelu(x, approximate=True)

def _silu(x):
    return jax.nn.silu(x)

def _sigmoid(x):
    return jax.nn.sigmoid(x)

def _layernorm(x, axis=-1, eps=1e-05):
    m = jnp.mean(x, axis=axis, keepdims=True)
    v = jnp.var(x, axis=axis, keepdims=True)
    return (x - m) / jnp.sqrt(v + eps)

def _scatter_add(tgt, idx, src, axis=0):
    return tgt.at[idx].add(src)

def _segment_sum(src, seg, n):
    return jax.ops.segment_sum(src, seg, n)
kernel_name = 'mk_adaln_ffn_d1_seqx_r2_4e4282'

def setup_inputs(seed: int=0):
    np.random.seed(seed)
    _w = jnp.asarray

    def _rec_inputs():
        import jax
        import jax.numpy as jnp
        _rk = jax.random.key(seed)
        x = -0.0003929 + 0.9999 * jax.random.normal(jax.random.fold_in(_rk, 1), (8, 512, 512), jnp.float32)
        _lenS = 512 - jax.random.randint(jax.random.fold_in(_rk, 7), (8,), 0, max(1, 512 // 4) + 1, jnp.int32)
        _lenS2 = 512 - jax.random.randint(jax.random.fold_in(_rk, 8), (8,), 0, max(1, 512 // 4) + 1, jnp.int32)
        cond_256 = -0.0209273 + 1.04763 * jax.random.normal(jax.random.fold_in(_rk, 11), (8, 128), jnp.float32)
        return (x, cond_256)
    x, cond_256 = _rec_inputs()

    def _L0_cond_setup():
        import jax, jax.numpy as jnp
        import numpy as np
        EPS = 1e-08

        def hamilton(q1, q2):
            w1, x1, y1, z1 = (q1[..., i, :] for i in range(4))
            w2, x2, y2, z2 = (q2[..., i, :] for i in range(4))
            w = w1 * w2 - x1 * x2 - y1 * y2 - z1 * z2
            x = w1 * x2 + x1 * w2 + y1 * z2 - z1 * y2
            y = w1 * y2 - x1 * z2 + y1 * w2 + z1 * x2
            z = w1 * z2 + x1 * y2 - y1 * x2 + z1 * w2
            return jnp.stack([w, x, y, z], axis=-2)

        def _normalize(q):
            return q / jnp.sqrt(jnp.sum(q * q, axis=0, keepdims=True) + EPS)
        key = jax.random.key(seed)
        k1, k2, k3, k4 = jax.random.split(key, 4)
        B, T, d_model = (4, 2048, 512)
        quat_dim = d_model // 4
        x = jax.random.normal(k1, (B, T, d_model), dtype=jnp.float32)
        q_left = jax.random.normal(k2, (4, quat_dim), dtype=jnp.float32)
        q_right = jax.random.normal(k3, (4, quat_dim), dtype=jnp.float32)
        spectral_gate = jax.random.uniform(k4, (1, 1, 1, quat_dim), dtype=jnp.float32)
        return {'x': x, 'q_left': q_left, 'q_right': q_right, 'spectral_gate': spectral_gate}
    _L0_cond_all = _L0_cond_setup()
    _L0_cond_in = {k: v for k, v in _L0_cond_all.items() if k in ('q_right', 'spectral_gate')}
    del _L0_cond_all

    def _L0_ffn_setup():
        import math
        import jax, jax.numpy as jnp
        import numpy as np
        D_MODEL = 512
        NUM_EXPERTS = 8
        D_FF_EXPERT = max(64, int(D_MODEL * 4 * 0.25))
        THRESHOLD = 0.9
        CAP_FACTOR = 1.0
        INIT_STD = 0.02

        def _xmoe_route(probs):
            N, E = probs.shape
            order = jnp.argsort(-probs, axis=-1)
            p_sorted = jnp.take_along_axis(probs, order, axis=-1)
            csum = jnp.cumsum(p_sorted, axis=-1)
            reached = (csum >= THRESHOLD).at[:, -1].set(True)
            k_idx = jnp.argmax(reached, axis=-1)
            select_prefix = jnp.arange(E)[None, :] <= k_idx[:, None]
            rows = jnp.arange(N)[:, None]
            assign_mask = jnp.zeros((N, E), dtype=bool).at[rows, order].set(select_prefix)
            rank = jnp.arange(1, E + 1, dtype=probs.dtype)[None, :]
            R_sorted = jnp.where(select_prefix, p_sorted - rank, jnp.full_like(p_sorted, -1000000000.0))
            R = jnp.zeros((N, E), dtype=probs.dtype).at[rows, order].set(R_sorted)
            capacity = int(math.ceil(N / E) * CAP_FACTOR)
            C = min(capacity, N)
            tok_order = jnp.argsort(-R, axis=0)
            topC = tok_order[:C, :]
            keep = jnp.zeros((N, E), dtype=bool).at[topC, jnp.arange(E)[None, :]].set(True)
            final_mask = assign_mask & keep
            return jnp.where(final_mask, probs, jnp.zeros_like(probs))
        key = jax.random.key(seed)
        k_x, k_g, k_w1, k_w2 = jax.random.split(key, 4)
        B, T = (4, 1024)
        x = jax.random.normal(k_x, (B, T, D_MODEL), dtype=jnp.float32)
        bound = 1.0 / math.sqrt(D_MODEL)
        gate_w = jax.random.uniform(k_g, (NUM_EXPERTS, D_MODEL), minval=-bound, maxval=bound, dtype=jnp.float32)
        w1 = INIT_STD * jax.random.normal(k_w1, (NUM_EXPERTS, D_FF_EXPERT, D_MODEL), dtype=jnp.float32)
        w2 = INIT_STD * jax.random.normal(k_w2, (NUM_EXPERTS, D_MODEL, D_FF_EXPERT), dtype=jnp.float32)
        return {'x': x, 'gate_w': gate_w, 'w1': w1, 'w2': w2}
    _L0_ffn_all = _L0_ffn_setup()
    _L0_ffn_in = {k: v for k, v in _L0_ffn_all.items() if k in ('gate_w', 'w1', 'w2')}
    del _L0_ffn_all
    return {'x': x, 'cond_256': cond_256, 'L0_cond_q_right': _L0_cond_in['q_right'], 'L0_cond_spectral_gate': _L0_cond_in['spectral_gate'], 'L0_ffn_gate_w': _L0_ffn_in['gate_w'], 'L0_ffn_w1': _L0_ffn_in['w1'], 'L0_ffn_w2': _L0_ffn_in['w2']}

def reference(x, cond_256, L0_cond_q_right, L0_cond_spectral_gate, L0_ffn_gate_w, L0_ffn_w1, L0_ffn_w2):
    import jax
    import jax.numpy as jnp

    def _L0_cond_ref(x, q_left, q_right, spectral_gate):
        import jax, jax.numpy as jnp
        import numpy as np
        EPS = 1e-08

        def hamilton(q1, q2):
            w1, x1, y1, z1 = (q1[..., i, :] for i in range(4))
            w2, x2, y2, z2 = (q2[..., i, :] for i in range(4))
            w = w1 * w2 - x1 * x2 - y1 * y2 - z1 * z2
            x = w1 * x2 + x1 * w2 + y1 * z2 - z1 * y2
            y = w1 * y2 - x1 * z2 + y1 * w2 + z1 * x2
            z = w1 * z2 + x1 * y2 - y1 * x2 + z1 * w2
            return jnp.stack([w, x, y, z], axis=-2)

        def _normalize(q):
            return q / jnp.sqrt(jnp.sum(q * q, axis=0, keepdims=True) + EPS)
        B, T, d_model = x.shape
        quat_dim = d_model // 4
        x_quat = x.reshape(B, T, 4, quat_dim)
        x_spectral = jnp.fft.fft(x_quat, axis=1)
        x_filtered = jnp.fft.ifft(x_spectral * spectral_gate, axis=1).real.astype(x.dtype)
        q_left_n = _normalize(q_left)
        q_right_n = _normalize(q_right)
        conj_sign = jnp.array([1.0, -1.0, -1.0, -1.0], dtype=x.dtype)[:, None]
        q_right_conj = q_right_n * conj_sign
        x_right = hamilton(x_filtered, q_right_conj)
        x_rotated = hamilton(q_left_n, x_right)
        return x_rotated.reshape(B, T, d_model)

    def _L0_ffn_ref(x, gate_w, w1, w2):
        import math
        import jax, jax.numpy as jnp
        import numpy as np
        D_MODEL = 512
        NUM_EXPERTS = 8
        D_FF_EXPERT = max(64, int(D_MODEL * 4 * 0.25))
        THRESHOLD = 0.9
        CAP_FACTOR = 1.0
        INIT_STD = 0.02

        def _xmoe_route(probs):
            N, E = probs.shape
            order = jnp.argsort(-probs, axis=-1)
            p_sorted = jnp.take_along_axis(probs, order, axis=-1)
            csum = jnp.cumsum(p_sorted, axis=-1)
            reached = (csum >= THRESHOLD).at[:, -1].set(True)
            k_idx = jnp.argmax(reached, axis=-1)
            select_prefix = jnp.arange(E)[None, :] <= k_idx[:, None]
            rows = jnp.arange(N)[:, None]
            assign_mask = jnp.zeros((N, E), dtype=bool).at[rows, order].set(select_prefix)
            rank = jnp.arange(1, E + 1, dtype=probs.dtype)[None, :]
            R_sorted = jnp.where(select_prefix, p_sorted - rank, jnp.full_like(p_sorted, -1000000000.0))
            R = jnp.zeros((N, E), dtype=probs.dtype).at[rows, order].set(R_sorted)
            capacity = int(math.ceil(N / E) * CAP_FACTOR)
            C = min(capacity, N)
            tok_order = jnp.argsort(-R, axis=0)
            topC = tok_order[:C, :]
            keep = jnp.zeros((N, E), dtype=bool).at[topC, jnp.arange(E)[None, :]].set(True)
            final_mask = assign_mask & keep
            return jnp.where(final_mask, probs, jnp.zeros_like(probs))
        B, T, D = x.shape
        N = B * T
        xf = x.reshape(N, D)
        probs = jax.nn.softmax(xf @ gate_w.T, axis=-1)
        scores_sel = _xmoe_route(probs)
        h = jax.nn.gelu(jnp.einsum('nd,efd->enf', xf, w1), approximate=False)
        y_e = jnp.einsum('enf,edf->end', h, w2)
        y = jnp.einsum('ne,end->nd', scores_sel, y_e)
        return y.reshape(B, T, D)
    x = x + _L0_ffn_ref(_L0_cond_ref(x, cond_256, L0_cond_q_right, L0_cond_spectral_gate), L0_ffn_gate_w, L0_ffn_w1, L0_ffn_w2)
    return x

_drawn_inputs = setup_inputs


def setup_inputs(seed=0):
    import zlib

    import numpy as np

    out = dict(_drawn_inputs(seed))
    spreads = {}
    factors = {'cond_256': 7.649,
     'L0_cond_q_right': 7.571,
     'L0_cond_spectral_gate': 8.0,
     'L0_ffn_gate_w': 8.0,
     'L0_ffn_w1': 7.603,
     'L0_ffn_w2': 7.558}
    for name, (base, spread) in spreads.items():
        noise = np.random.default_rng([zlib.crc32(name.encode()), seed]).standard_normal(out[name].shape)
        drawn = base * np.exp(spread * noise) if base else spread * noise
        out[name] = jnp.asarray(drawn.astype(out[name].dtype))
    for name, factor in factors.items():
        out[name] = (out[name] * factor).astype(out[name].dtype)
    return out
```

```python
import numpy as np
from contextlib import ExitStack

import concourse.bass as bass
from concourse import mybir

FP32 = mybir.dt.float32
F32R = mybir.dt.float32r
FP16 = mybir.dt.float16
U32 = mybir.dt.uint32
I32 = mybir.dt.int32
ALU = mybir.AluOpType
ACT = mybir.ActivationFunctionType
AX = mybir.AxisListType

P = 128
B, T_SEQ, D = 8, 512, 512
N = B * T_SEQ
NT = N // P
E, F = 8, 512
CAP = N // E
C4 = D // P
F4 = F // P
S4 = CAP // P
TG = 512
NG = N // TG
XRING = 4
KV, KA = 4, 3
KT = KV + KA
ROUNDS = 8
TC = P // E
KEY_MID = 0.5
NA, NB = 32, 16
SPARE = CAP
NEPS = 1e-8
THRESHOLD = 0.9
KEY_ULP = 2.0 ** -24
FILLED = -6144.0
EMPTY = 8192.0
CF, NCF = {}, 0
for _name, _width in (("ident", P), ("sel", E), ("octet", NA), ("spare", S4), ("start", KT), ("need", KT),
                      ("step", ROUNDS * KT), ("offset", ROUNDS * KT)):
    CF[_name] = (NCF, NCF + _width)
    NCF += _width
CH = dict(tok=(0, NT), iota=(NT, NT + NA), spread=(NT + NA, NT + NA + P), ones=(NT + NA + P, NT + NA + 2 * P),
          chunks=(NT + NA + 2 * P, NT + NA + 3 * P), lower=(NT + NA + 3 * P, NT + NA + 4 * P))
NCH = CH["lower"][1]
NQ = 8 + 4 + 1 + C4 * E

SA = [[1, -1, -1, -1], [1, 1, -1, 1], [1, 1, 1, -1], [1, -1, 1, 1]]
SB = [[1, 1, 1, 1], [-1, 1, -1, 1], [-1, 1, 1, -1], [-1, -1, 1, 1]]


def build(nc, xt_d, x_d, small_d, w1_d, w2_d, cf_d, ch_d, out_d):
    probs_d = nc.dram_tensor("probs_scratch", (N * E, 1), FP32, kind="Internal").ap()
    ctx = ExitStack()
    with ctx:
        ctx.enter_context(nc.allow_low_precision(reason="counts up to 256 are exact in float16"))

        def sb(name, shape, dt=FP32):
            return ctx.enter_context(nc.sbuf_tensor(name, shape, dt))

        def sem(name):
            return ctx.enter_context(nc.semaphore(name))

        cf = sb("cf", [P, NCF])
        ch = sb("ch", [P, NCH], FP16)
        small = sb("small", [P, NQ])
        cfv = lambda k: cf[:, CF[k][0]:CF[k][1]]
        chv = lambda k: ch[:, CH[k][0]:CH[k][1]]

        sq = sb("sq", [P, 12])
        nrm = sb("nrm", [P, 8])
        qn = sb("qn", [P, 8])
        rotA = sb("rotA", [P, 4, 4])
        rotB = sb("rotB", [P, 4, 4])
        rot = sb("rot", [P, 4, 4])
        rtmp = sb("rtmp", [P, 4, 4])
        gfold = sb("gfold", [P, C4, E])
        gtmp = sb("gtmp", [P, C4, E])

        region = sb("region", [P, XRING * C4 * TG])
        xt = region[:, :].rearrange("p (r c n) -> p r c n", r=XRING, c=C4)
        before = region[:, 0:NT * E * E].rearrange("p (t e f) -> p t e f", e=E, f=E)
        mass = region[:, NT * E * E:2 * NT * E * E].rearrange("p (t e f) -> p t e f", e=E, f=E)
        lev = sb("lev", [P, E, NT * E], FP16)
        tk = lambda name: sb(name, [P, NT, E])
        cent, prob, rank, csum, arank, key = (tk(n) for n in ("cent", "prob", "rank", "csum", "arank", "key"))
        rmax = sb("rmax", [P, NT])
        rsum = sb("rsum", [P, NT])
        lowlev = sb("lowlev", [P, E, E])
        rstar = sb("rstar", [P, E])
        keys = sb("keys", [P, N // TC])
        hits = region[:, 0:KT * N // TC // 2].bitcast(FP16).rearrange("p (k n) -> p k n", k=KT)
        base = sb("base", [P, 2, KT])
        thr = sb("thr", [P, 2, KT])
        nxt = sb("nxt", [P, KT])
        cnt = sb("cnt", [P, 2, KT], FP16)
        passed = sb("passed", [P, KT])
        best = sb("best", [P, 1])
        tb = sb("tb", [P, E])
        mask = sb("mask", [P, 2, E, NT], FP16)
        seg = sb("seg", [P, 2 * E * NT])
        places = region[:, N // 2:N].rearrange("p (q e t) -> p q e t", e=E, t=NT)
        incl, pos, posi, pab = places[:, 0:2], places[:, 2:4], places[:, 4].bitcast(I32), places[:, 5:7].bitcast(I32)
        ab = sb("ab", [P, 2, E, NT], FP16)
        hotA = sb("hotA", [P, NT, NA], FP16)
        hotB = sb("hotB", [P, NT, 2 * NB], FP16)
        tabU = sb("tabU", [2 * NB, NA], FP16)
        tabV = sb("tabV", [P, NA])
        tabf = sb("tabf", [P, S4])
        scat = sb("scat", [P, E, S4], U32)
        gath = sb("gath", [P, E, S4], U32)
        pidx = sb("pidx", [P, E, S4], U32)
        ptmp = sb("ptmp", [P, 2, S4], U32)

        w1raw = sb("w1raw", [P, 2, C4, F])
        w2raw = sb("w2raw", [P, F4, D])
        w1rot = sb("w1rot", [P, C4, F])
        w1h = [sb(f"w1h{i}", [P, C4, F], F32R) for i in range(2)]
        w1l = [sb(f"w1l{i}", [P, C4, F], F32R) for i in range(2)]
        w2h = [sb(f"w2h{i}", [P, F4, D], F32R) for i in range(2)]
        w2l = [sb(f"w2l{i}", [P, F4, D], F32R) for i in range(2)]
        xg = sb("xg", [P, S4, D])
        xh = sb("xh", [P, C4, CAP], F32R)
        xl = sb("xl", [P, C4, CAP], F32R)
        hf = sb("hf", [P, 2, CAP])
        hh = sb("hh", [P, F4, CAP], F32R)
        hl = sb("hl", [P, F4, CAP], F32R)
        score = sb("score", [P, 2, S4])
        ysb = sb("ysb", [P, S4, D])

        bank = [ctx.enter_context(nc.psum_tensor(f"bank{i}", [P, 512], FP32)) for i in range(8)]
        xbank, hbank, ybank = bank[0:2], bank[2:4], bank[4:6]
        ubank, vbank = bank[6], bank[7]

        small_in, cf_in, ch_in = sem("small_in"), sem("cf_in"), sem("ch_in")
        xt_in = [sem(f"xt_in{i}") for i in range(XRING)]
        w1_in = [sem(f"w1_in{i}") for i in range(2)]
        w2_in = sem("w2_in")
        out_base, probs_out = sem("out_base"), sem("probs_out")
        squares, roots = sem("squares"), sem("roots")
        gate_folded, logits_mm = sem("gate_folded"), sem("logits_mm")
        dve_step = sem("dve_step")
        centred, exped, prob_ready = sem("centred"), sem("exped"), sem("prob_ready")
        lev_ready, lev_mm = sem("lev_ready"), sem("lev_mm")
        key_ready, key_mm = sem("key_ready"), sem("key_mm")
        thr_ready, cnt_v, cnt_a, cnt_mm = sem("thr_ready"), sem("cnt_v"), sem("cnt_a"), sem("cnt_mm")
        base_ready, tb_mm = sem("base_ready"), sem("tb_mm")
        mask_ready, prefix_mm = sem("mask_ready"), sem("prefix_mm")
        hot_ready, u_mm, u_ev, v_mm, slots_ready = (sem(n) for n in ("hot_ready", "u_mm", "u_ev", "v_mm", "slots_ready"))
        xg_in = sem("xg_in")
        score_in = [sem(f"score_in{i}") for i in range(2)]
        xt_mm, x_hi, x_lo = sem("xt_mm"), sem("x_hi"), sem("x_lo")
        w1_rot, w1_hi, w1_lo = sem("w1_rot"), sem("w1_hi"), sem("w1_lo")
        w2_hi, w2_lo = sem("w2_hi"), sem("w2_lo")
        h_mm, h_act, h_hi, h_lo = sem("h_mm"), sem("h_act"), sem("h_hi"), sem("h_lo")
        y_mm, y_ev = sem("y_mm"), sem("y_ev")
        added = [sem(f"added{i}") for i in range(S4)]

        block = ctx.enter_context(nc.Block())

        @block.sync
        def _(sp):
            sp.dma_start(small[:, :], small_d).then_inc(small_in, 16)

            def load_x(g):
                if g >= XRING:
                    sp.wait_ge(logits_mm, g - XRING + 1)
                sp.dma_start(xt[:, g % XRING], xt_d[g]).then_inc(xt_in[g % XRING], 16)

            def load_w1(e):
                if e >= 2:
                    sp.wait_ge(w1_rot, C4 * (e - 1))
                sp.dma_start(w1raw[:, e % 2], w1_d[e]).then_inc(w1_in[e % 2], 16)

            def load_w2(e):
                if e >= 1:
                    sp.wait_ge(w2_lo, e)
                sp.dma_start(w2raw[:, :, :], w2_d[e]).then_inc(w2_in, 16)

            for g in range(NG // 2):
                load_x(g)
            load_w1(0)
            for g in range(NG // 2, NG):
                load_x(g)
            sp.dma_start(ch[:, :], ch_d).then_inc(ch_in, 16)
            sp.dma_start(cf[:, :], cf_d).then_inc(cf_in, 16)
            load_w1(1)
            load_w2(0)
            sp.dma_start(out_d[0:N, :], x_d).then_inc(out_base, 16)
            sp.dma_start(out_d[N:N + SPARE, :], x_d[0:SPARE, :]).then_inc(out_base, 16)
            sp.wait_ge(prob_ready, 1)
            sp.dma_start(probs_d.rearrange("(p n) o -> p (n o)", p=P),
                         prob[:, :, :].rearrange("p t e -> p (t e)")).then_inc(probs_out, 16)
            for e in range(1, E):
                load_w2(e)
                if e + 1 < E:
                    load_w1(e + 1)
            for s in range(S4):
                sp.wait_ge(added[s], 16 * E)

        @block.gpsimd
        def _(pool):
            def gather(e):
                pool.wait_ge(slots_ready, e + 1)
                if e >= 1:
                    pool.wait_ge(xt_mm, C4 * e)
                for s in range(S4):
                    pool.indirect_dma_start(xg[:, s, :], None, x_d,
                                            bass.IndirectOffsetOnAxis(gath[:, e, s:s + 1], 0)).then_inc(xg_in, 16)
                for s in range(S4):
                    pool.indirect_dma_start(score[:, e % 2, s:s + 1], None, probs_d,
                                            bass.IndirectOffsetOnAxis(pidx[:, e, s:s + 1], 0)).then_inc(score_in[e % 2], 16)

            def scatter(e):
                for s in range(S4):
                    if e >= 1:
                        pool.wait_ge(added[s], 16 * e)
                for s in range(S4):
                    pool.wait_ge(y_ev, S4 * e + s + 1)
                    pool.indirect_dma_start(out_d, bass.IndirectOffsetOnAxis(scat[:, e, s:s + 1], 0),
                                            ysb[:, s, :], None, compute_op=ALU.add).then_inc(added[s], 16)

            pool.wait_ge(probs_out, 16)
            gather(0)
            for e in range(E):
                if e + 1 < E:
                    gather(e + 1)
                if e == 0:
                    pool.wait_ge(out_base, 32)
                scatter(e)

        @block.scalar
        def _(act):
            act.wait_ge(squares, 1)
            nc.scalar.activation(nrm[:, 2:4], nrm[:, 0:2], ACT.Sqrt).then_inc(roots, 1)

            def w1_high(e, j):
                act.wait_ge(w1_rot, C4 * e + j + 1)
                if e >= 2:
                    act.wait_ge(h_mm, F4 * (e - 1))
                nc.scalar.activation(w1h[e % 2][:, j, :], w1rot[:, j, :], ACT.Copy).then_inc(w1_hi, 1)

            def w2_high(e):
                act.wait_ge(w2_in, 16 * (e + 1))
                if e >= 2:
                    act.wait_ge(y_mm, S4 * (e - 1))
                nc.scalar.activation(w2h[e % 2][:, :, :], w2raw[:, :, :], ACT.Copy).then_inc(w2_hi, 1)

            def x_high(e):
                for j in range(C4):
                    act.wait_ge(xt_mm, C4 * e + j + 1)
                    nc.scalar.activation(xh[:, j, :], xbank[j % 2][:, :], ACT.Copy).then_inc(x_hi, 1)

            def hidden(e, f):
                n = F4 * e + f
                act.wait_ge(h_mm, n + 1)
                if n >= 2:
                    act.wait_ge(h_lo, n - 1)
                nc.scalar.activation(hf[:, n % 2, :], hbank[n % 2][:, :], ACT.Gelu).then_inc(h_act, 1)
                act.wait_ge(h_act, n + 1)
                if e >= 1:
                    act.wait_ge(y_mm, S4 * e)
                nc.scalar.activation(hh[:, f, :], hf[:, n % 2, :], ACT.Copy).then_inc(h_hi, 1)

            def y_out(e, s):
                n = S4 * e + s
                act.wait_ge(y_mm, n + 1)
                if s == 0:
                    act.wait_ge(score_in[e % 2], 16 * S4 * (e // 2 + 1))
                if e >= 1:
                    act.wait_ge(added[s], 16 * e)
                nc.scalar.activation(ysb[:, s, :], ybank[n % 2][:, :], ACT.Copy,
                                     scale=score[:, e % 2, s:s + 1]).then_inc(y_ev, 1)

            for j in range(C4):
                w1_high(0, j)
            act.wait_ge(centred, 1)
            nc.scalar.activation(cent[:, :, :], cent[:, :, :], ACT.Exp).then_inc(exped, 1)
            w2_high(0)
            for r in range(ROUNDS):
                act.wait_ge(thr_ready, r + 1)
                if r >= 2:
                    act.wait_ge(cnt_mm, r - 1)
                for k in range(KV, KT):
                    last = nc.scalar.activation(hits[:, k, :], keys[:, :], ACT.Sign, bias=thr[:, r % 2, k:k + 1],
                                                accum_out=cnt[:, r % 2, k:k + 1])
                last.then_inc(cnt_a, 1)
            x_high(0)
            for e in range(E):
                for f in range(F4):
                    hidden(e, f)
                if e + 1 < E:
                    for j in range(C4 - 1):
                        w1_high(e + 1, j)
                    x_high(e + 1)
                    w1_high(e + 1, C4 - 1)
                y_out(e, 0)
                if e + 1 < E:
                    w2_high(e + 1)
                for s in range(1, S4):
                    y_out(e, s)

        @block.vector
        def _(dve):
            steps = [0]

            def then(ins):
                steps[0] += 1
                ins.then_inc(dve_step, 1)
                dve.wait_ge(dve_step, steps[0])

            def rotate_w1(e, j):
                if j == 0:
                    dve.wait_ge(w1_in[e % 2], 16 * (e // 2 + 1))
                    if e >= 1:
                        dve.wait_ge(w1_lo, e)
                dst = w1rot[:, j, :]
                then(nc.vector.tensor_scalar(dst, w1raw[:, e % 2, 0, :], rot[:, 0, j:j + 1], None, ALU.mult))
                for i in range(1, C4):
                    ins = nc.vector.scalar_tensor_tensor(dst, w1raw[:, e % 2, i, :], rot[:, i, j:j + 1], dst,
                                                         ALU.mult, ALU.add)
                    if i < C4 - 1:
                        then(ins)
                ins.then_inc(w1_rot, 1)

            def w1_low(e):
                dve.wait_ge(w1_hi, C4 * (e + 1))
                nc.vector.tensor_tensor(w1l[e % 2][:, :, :], w1rot[:, :, :], w1h[e % 2][:, :, :].bitcast(FP32),
                                        ALU.subtract).then_inc(w1_lo, 1)

            def w2_low(e):
                dve.wait_ge(w2_hi, e + 1)
                nc.vector.tensor_tensor(w2l[e % 2][:, :, :], w2raw[:, :, :], w2h[e % 2][:, :, :].bitcast(FP32),
                                        ALU.subtract).then_inc(w2_lo, 1)

            def x_low(e):
                for j in range(C4):
                    dve.wait_ge(x_hi, C4 * e + j + 1)
                    nc.vector.tensor_tensor(xl[:, j, :], xbank[j % 2][:, :], xh[:, j, :].bitcast(FP32),
                                            ALU.subtract).then_inc(x_lo, 1)

            def h_low(e, f):
                n = F4 * e + f
                dve.wait_ge(h_hi, n + 1)
                nc.vector.tensor_tensor(hl[:, f, :], hf[:, n % 2, :], hh[:, f, :].bitcast(FP32),
                                        ALU.subtract).then_inc(h_lo, 1)

            def one_hots(e):
                if e >= 1:
                    dve.wait_ge(u_mm, e)
                nc.vector.tensor_tensor(hotA[:, :, :], ab[:, 0, e, :].unsqueeze(2).to_broadcast([P, NT, NA]),
                                        chv("iota").unsqueeze(1).to_broadcast([P, NT, NA]), ALU.is_equal)
                then(nc.vector.tensor_tensor(hotB[:, :, NB:], ab[:, 1, e, :].unsqueeze(2).to_broadcast([P, NT, NB]),
                                             chv("iota")[:, 0:NB].unsqueeze(1).to_broadcast([P, NT, NB]), ALU.is_equal))
                nc.vector.tensor_tensor(hotB[:, :, 0:NB], hotB[:, :, NB:],
                                        chv("tok").unsqueeze(2).to_broadcast([P, NT, NB]), ALU.mult).then_inc(hot_ready, 1)

            def table_rows(e):
                dve.wait_ge(u_mm, e + 1)
                nc.vector.tensor_copy(tabU[:, :], ubank[0:2 * NB, 0:NA]).then_inc(u_ev, 1)

            def slot_tables(e):
                dve.wait_ge(v_mm, e + 1)
                then(nc.vector.tensor_tensor(tabV[:, :], vbank[:, 0:NA], cfv("octet"), ALU.mult))
                then(nc.vector.tensor_reduce(tabf[:, :], tabV[:, :].rearrange("p (g c) -> p c g", c=S4), AX.X, ALU.add))
                nc.vector.scalar_tensor_tensor(scat[:, e, :], tabf[:, :], EMPTY, cfv("spare"), ALU.add, ALU.min)
                then(nc.vector.tensor_scalar(tabV[:, 0:S4], tabf[:, :], EMPTY, float(N - 1), ALU.add, ALU.min))
                then(nc.vector.tensor_copy(gath[:, e, :], tabV[:, 0:S4]))
                nc.vector.tensor_scalar(ptmp[:, 0, :], gath[:, e, :], P - 1, 8, ALU.bitwise_and, ALU.logical_shift_left)
                then(nc.vector.tensor_scalar(ptmp[:, 1, :], gath[:, e, :], 7, 3, ALU.logical_shift_right,
                                             ALU.logical_shift_left))
                nc.vector.scalar_tensor_tensor(pidx[:, e, :], ptmp[:, 0, :], e, ptmp[:, 1, :], ALU.bitwise_or,
                                               ALU.bitwise_or).then_inc(slots_ready, 1)

            nc.vector.memset(seg[:, :], 1.0)
            dve.wait_ge(small_in, 16)
            then(nc.vector.tensor_tensor(sq[:, :], small[:, 0:12], small[:, 0:12], ALU.mult))
            nc.vector.tensor_reduce(nrm[:, 0:1], sq[:, 0:8], AX.X, ALU.add)
            then(nc.vector.tensor_reduce(nrm[:, 1:2], sq[:, 8:12], AX.X, ALU.add))
            nc.vector.tensor_scalar(nrm[:, 0:2], nrm[:, 0:2], NEPS, None, ALU.add).then_inc(squares, 1)
            dve.wait_ge(roots, 1)
            then(nc.vector.reciprocal(nrm[:, 4:6], nrm[:, 2:4]))
            then(nc.vector.tensor_tensor(nrm[:, 4:6], nrm[:, 4:6], nrm[:, 0:2], ALU.mult))
            then(nc.vector.tensor_tensor(nrm[:, 4:6], nrm[:, 4:6], nrm[:, 2:4], ALU.add))
            then(nc.vector.tensor_scalar(nrm[:, 4:6], nrm[:, 4:6], 0.5, None, ALU.mult))
            then(nc.vector.reciprocal(nrm[:, 6:8], nrm[:, 4:6]))
            nc.vector.tensor_scalar(qn[:, 0:4], small[:, 0:4], nrm[:, 6:7], None, ALU.mult)
            then(nc.vector.tensor_scalar(qn[:, 4:8], small[:, 8:12], nrm[:, 7:8], None, ALU.mult))
            for i in range(4):
                for k in range(4):
                    nc.vector.tensor_scalar(rotA[:, i, k:k + 1], qn[:, i ^ k:(i ^ k) + 1], float(SA[i][k]), None, ALU.mult)
                    last = nc.vector.tensor_scalar(rotB[:, i, k:k + 1], qn[:, 4 + (i ^ k):5 + (i ^ k)],
                                                   float(SB[i][k]), small[:, 12:13], ALU.mult, ALU.mult)
            then(last)
            for k in range(4):
                dst = rot if k == 0 else rtmp
                then(nc.vector.tensor_tensor(dst[:, :, :], rotA[:, :, k].unsqueeze(2).to_broadcast([P, 4, 4]),
                                             rotB[:, k, :].unsqueeze(1).to_broadcast([P, 4, 4]), ALU.mult))
                if k:
                    then(nc.vector.tensor_tensor(rot[:, :, :], rot[:, :, :], rtmp[:, :, :], ALU.add))
            gw = small[:, 13:NQ].rearrange("p (c e) -> p c e", e=E)
            for i in range(C4):
                dst = gfold if i == 0 else gtmp
                then(nc.vector.tensor_tensor(dst[:, :, :], rot[:, i, :].unsqueeze(2).to_broadcast([P, C4, E]),
                                             gw[:, i, :].unsqueeze(1).to_broadcast([P, C4, E]), ALU.mult))
                if i:
                    ins = nc.vector.tensor_tensor(gfold[:, :, :], gfold[:, :, :], gtmp[:, :, :], ALU.add)
                    if i < C4 - 1:
                        then(ins)
            ins.then_inc(gate_folded, 1)
            nc.vector.memset(seg[:, :].rearrange("p (g t) -> p g t", t=NT)[:, :, 0:1], 0.0)

            for j in range(C4):
                rotate_w1(0, j)
            w1_low(0)

            dve.wait_ge(logits_mm, NG)
            logits = bank[0][:, 0:NT * E].rearrange("p (t e) -> p t e", e=E)
            then(nc.vector.tensor_reduce(rmax[:, :], logits, AX.X, ALU.max))
            nc.vector.tensor_tensor(cent[:, :, :], logits, rmax[:, :].unsqueeze(2).to_broadcast([P, NT, E]),
                                    ALU.subtract).then_inc(centred, 1)
            nc.vector.memset(before, 0.0)
            dve.wait_ge(exped, 1)
            then(nc.vector.tensor_reduce(rsum[:, :], cent[:, :, :], AX.X, ALU.add))
            then(nc.vector.reciprocal(rsum[:, :], rsum[:, :]))
            nc.vector.tensor_tensor(prob[:, :, :], cent[:, :, :], rsum[:, :].unsqueeze(2).to_broadcast([P, NT, E]),
                                    ALU.mult).then_inc(prob_ready, 1)
            dve.wait_ge(prob_ready, 1)

            for e in range(E):
                for lo, hi, op in ((0, e, ALU.is_ge), (e + 1, E, ALU.is_gt)):
                    if lo < hi:
                        last = nc.vector.tensor_tensor(before[:, :, e, lo:hi], prob[:, :, lo:hi],
                                                       prob[:, :, e:e + 1].to_broadcast([P, NT, hi - lo]), op)
            then(last)
            nc.vector.tensor_reduce(rank[:, :, :], before, AX.X, ALU.add)
            for e in range(E):
                last = nc.vector.tensor_tensor(mass[:, :, e, :], before[:, :, e, :], prob[:, :, :], ALU.mult)
            then(last)
            then(nc.vector.tensor_reduce(csum[:, :, :], mass, AX.X, ALU.add))
            nc.vector.tensor_scalar(csum[:, :, :], csum[:, :, :], THRESHOLD, 16.0, ALU.is_ge, ALU.mult)
            then(nc.vector.tensor_scalar(rank[:, :, :], rank[:, :, :], 1.0, None, ALU.add))
            then(nc.vector.tensor_tensor(arank[:, :, :], rank[:, :, :], csum[:, :, :], ALU.add))
            flat = arank[:, :, :].rearrange("p t e -> p (t e)")
            for r in range(E):
                last = nc.vector.tensor_scalar(lev[:, r, :], flat, float(r + 1), None, ALU.is_le)
            last.then_inc(lev_ready, 1)
            then(nc.vector.tensor_tensor(key[:, :, :], prob[:, :, :], rank[:, :, :], ALU.subtract))
            nc.vector.tensor_tensor(key[:, :, :], key[:, :, :], rank[:, :, :], ALU.add)
            then(nc.vector.tensor_scalar(csum[:, :, :], rank[:, :, :], 1.0, KEY_ULP, ALU.is_equal, ALU.mult))
            then(nc.vector.scalar_tensor_tensor(key[:, :, :], key[:, :, :], KEY_MID, csum[:, :, :], ALU.subtract, ALU.subtract))
            dve.wait_ge(lev_mm, 1)
            then(nc.vector.tensor_scalar(lowlev[:, :, :], bank[1][:, 0:E * E].rearrange("p (r e) -> p e r", e=E),
                                         float(CAP), None, ALU.is_lt))
            then(nc.vector.tensor_reduce(rstar[:, :], lowlev[:, :, :], AX.X, ALU.add))
            then(nc.vector.scalar_tensor_tensor(arank[:, :, :], rstar[:, :].unsqueeze(1).to_broadcast([P, NT, E]), 1.0,
                                                arank[:, :, :], ALU.add, ALU.subtract))
            then(nc.vector.scalar_tensor_tensor(key[:, :, :], arank[:, :, :], 4.0, key[:, :, :], ALU.mult, ALU.add))
            nc.vector.tensor_scalar(key[:, :, :], key[:, :, :], 2.0, -1.0, ALU.min, ALU.max).then_inc(key_ready, 1)
            dve.wait_ge(cf_in, 16)
            table = lambda k, r: cfv(k)[:, r * KT:(r + 1) * KT]
            nc.vector.tensor_copy(base[:, 0, :], cfv("start"))
            dve.wait_ge(key_mm, 1)
            nc.vector.tensor_copy(keys[:, :], bank[0][:, 0:N // TC])
            nc.vector.tensor_tensor(thr[:, 0, :], cfv("start"), table("offset", 0), ALU.add).then_inc(thr_ready, 1)
            dve.wait_ge(thr_ready, 1)

            for r in range(ROUNDS):
                now, new = r % 2, (r + 1) % 2
                if r + 1 < ROUNDS:
                    nc.vector.tensor_tensor(nxt[:, :], base[:, now, :], table("offset", r + 1), ALU.add)
                if r >= 2:
                    dve.wait_ge(cnt_mm, r - 1)
                for k in range(KV):
                    last = nc.vector.tensor_scalar(hits[:, k, :], keys[:, :], thr[:, now, k:k + 1], None, ALU.is_ge, ALU.add,
                                                   accum_out=cnt[:, now, k:k + 1])
                last.then_inc(cnt_v, 1)
                dve.wait_ge(cnt_mm, r + 1)
                then(nc.vector.scalar_tensor_tensor(passed[:, :], bank[1 + now][:, 0:KT], 0.0, cfv("need"), ALU.add,
                                                    ALU.is_ge, accum_out=best[:, :]))
                if r + 1 < ROUNDS:
                    nc.vector.scalar_tensor_tensor(thr[:, new, :], table("step", r), best[:, :], nxt[:, :], ALU.mult,
                                                   ALU.add).then_inc(thr_ready, 1)
                ins = nc.vector.scalar_tensor_tensor(base[:, new, :], table("step", r), best[:, :], base[:, now, :],
                                                     ALU.mult, ALU.add)
                if r + 1 < ROUNDS:
                    then(ins)
            ins.then_inc(base_ready, 1)

            dve.wait_ge(tb_mm, 1)
            then(nc.vector.tensor_copy(tb[:, :], bank[5][:, 0:E]))
            for m, op in enumerate((ALU.is_gt, ALU.is_equal)):
                ins = nc.vector.tensor_tensor(mask[:, m, :, :].rearrange("p e t -> p t e"), key[:, :, :],
                                              tb[:, :].unsqueeze(1).to_broadcast([P, NT, E]), op)
            ins.then_inc(mask_ready, 1)
            dve.wait_ge(prefix_mm, 2)
            total = bank[4][:, :]
            fl = lambda x: x[:, :, :, :].rearrange("p m e t -> p (m e t)")
            then(nc.vector.tensor_tensor_scan(fl(incl), seg[:, :], total, 0.0, ALU.mult, ALU.add))
            then(nc.vector.tensor_tensor(fl(pos), fl(incl), total, ALU.subtract))
            then(nc.vector.tensor_tensor(fl(pos), fl(pos), bank[3][:, :], ALU.add))
            then(nc.vector.tensor_tensor(pos[:, 1], pos[:, 1], incl[:, 0, :, NT - 1:NT].to_broadcast([P, E, NT]), ALU.add))
            then(nc.vector.scalar_tensor_tensor(fl(pos), fl(pos), -2.0 * N, fl(mask), ALU.add, ALU.mult))
            then(nc.vector.tensor_tensor(pos[:, 0], pos[:, 0], pos[:, 1], ALU.add))
            then(nc.vector.tensor_scalar(posi[:, :, :], pos[:, 0], 2.0 * N, None, ALU.add))
            nc.vector.tensor_scalar(pab[:, 0], posi[:, :, :], 4, None, ALU.logical_shift_right)
            then(nc.vector.tensor_scalar(pab[:, 1], posi[:, :, :], NB - 1, None, ALU.bitwise_and))
            then(nc.vector.tensor_copy(fl(ab), fl(pab)))
            for e in range(2):
                one_hots(e)
                table_rows(e)
                slot_tables(e)

            w2_low(0)
            x_low(0)
            for e in range(E):
                more = e + 1 < E
                if e:
                    w2_low(e)
                if e + 2 < E:
                    one_hots(e + 2)
                for f in range(F4):
                    if more and f < C4 - 1:
                        rotate_w1(e + 1, f)
                    h_low(e, f)
                if more:
                    x_low(e + 1)
                if e + 2 < E:
                    table_rows(e + 2)
                if more:
                    rotate_w1(e + 1, C4 - 1)
                    w1_low(e + 1)
                if e + 2 < E:
                    slot_tables(e + 2)

        @block.tensor
        def _(pe):
            ident = cfv("ident")

            def slot_rows(e):
                pe.wait_ge(hot_ready, e + 1)
                if e >= 1:
                    pe.wait_ge(u_ev, e)
                for t in range(NT):
                    last = nc.tensor.matmul(ubank[0:2 * NB, 0:NA], hotB[:, t, :], hotA[:, t, :],
                                            start=(t == 0), stop=(t == NT - 1))
                last.then_inc(u_mm, 1)

            def slot_spread(e):
                pe.wait_ge(u_ev, e + 1)
                if e >= 1:
                    pe.wait_ge(slots_ready, e)
                nc.tensor.matmul(vbank[:, 0:NA], chv("spread")[0:2 * NB, :], tabU[:, :],
                                 start=True, stop=True).then_inc(v_mm, 1)

            def transpose_x(e):
                pe.wait_ge(xg_in, 16 * S4 * (e + 1))
                for j in range(C4):
                    n = C4 * e + j
                    if n >= 2:
                        pe.wait_ge(x_lo, n - 1)
                    for s in range(S4):
                        last = nc.tensor.transpose(xbank[j % 2][:, s * P:(s + 1) * P], xg[:, s, j * P:(j + 1) * P], ident)
                    last.then_inc(xt_mm, 1)

            def split_product(dst, pairs):
                for i, ((ah, al), (bh, bl)) in enumerate(pairs):
                    nc.tensor.matmul(dst, ah, bh, start=(i == 0), stop=False)
                    nc.tensor.matmul(dst, ah, bl, start=False, stop=False)
                    last = nc.tensor.matmul(dst, al, bh, start=False, stop=(i == len(pairs) - 1))
                return last

            def layer1(e):
                pe.wait_ge(w1_lo, e + 1)
                pe.wait_ge(x_lo, C4 * (e + 1))
                for f in range(F4):
                    n = F4 * e + f
                    if n >= 2:
                        pe.wait_ge(h_act, n - 1)
                    fs = slice(f * P, (f + 1) * P)
                    split_product(hbank[n % 2][:, :], [((w1h[e % 2][:, j, fs], w1l[e % 2][:, j, fs]), (xh[:, j, :], xl[:, j, :]))
                                                       for j in range(C4)]).then_inc(h_mm, 1)

            def layer2(e, blocks):
                pe.wait_ge(w2_lo, e + 1)
                pe.wait_ge(h_lo, F4 * (e + 1))
                for s in blocks:
                    n = S4 * e + s
                    if n >= 2:
                        pe.wait_ge(y_ev, n - 1)
                    ss = slice(s * P, (s + 1) * P)
                    split_product(ybank[n % 2][:, :], [((hh[:, f, ss], hl[:, f, ss]), (w2h[e % 2][:, f, :], w2l[e % 2][:, f, :]))
                                                       for f in range(F4)]).then_inc(y_mm, 1)

            pe.wait_ge(gate_folded, 1)
            for g in range(NG):
                pe.wait_ge(xt_in[g % XRING], 16 * (g // XRING + 1))
                for u in range(TG // P):
                    t = g * (TG // P) + u
                    for j in range(C4):
                        last = nc.tensor.matmul(bank[0][:, t * E:(t + 1) * E], xt[:, g % XRING, j, u * P:(u + 1) * P],
                                                gfold[:, j, :], start=(j == 0), stop=(j == C4 - 1))
                last.then_inc(logits_mm, 1)
            pe.wait_ge(ch_in, 16)
            pe.wait_ge(lev_ready, 1)
            for t in range(NT):
                last = nc.tensor.matmul(bank[1][:, 0:E * E], chv("ones"), lev[:, :, t * E:(t + 1) * E],
                                        start=(t == 0), stop=(t == NT - 1))
            last.then_inc(lev_mm, 1)
            pe.wait_ge(cf_in, 16)
            pe.wait_ge(key_ready, 1)
            for c in range(NT // TC):
                last = nc.tensor.transpose(bank[0][:, c * P:(c + 1) * P],
                                           key[:, c * TC:(c + 1) * TC, :].rearrange("p t e -> p (t e)"), ident)
            last.then_inc(key_mm, 1)
            for r in range(ROUNDS):
                pe.wait_ge(cnt_v, r + 1)
                pe.wait_ge(cnt_a, r + 1)
                nc.tensor.matmul(bank[1 + r % 2][:, 0:KT], chv("chunks"), cnt[:, r % 2, :],
                                 start=True, stop=True).then_inc(cnt_mm, 1)
            pe.wait_ge(base_ready, 1)
            nc.tensor.matmul(bank[5][:, 0:E], base[:, ROUNDS % 2, 0:1].to_broadcast([P, P]), cfv("sel"),
                             start=True, stop=True).then_inc(tb_mm, 1)
            pe.wait_ge(mask_ready, 1)
            masks = mask[:, :, :, :].rearrange("p m e t -> p (m e t)")
            nc.tensor.matmul(bank[3][:, :], chv("lower"), masks, start=True, stop=True).then_inc(prefix_mm, 1)
            nc.tensor.matmul(bank[4][:, :], chv("ones"), masks, start=True, stop=True).then_inc(prefix_mm, 1)
            for e in range(2):
                slot_rows(e)
                slot_spread(e)
            transpose_x(0)
            for e in range(E):
                layer1(e)
                if e + 1 < E:
                    transpose_x(e + 1)
                if e + 2 < E:
                    slot_rows(e + 2)
                layer2(e, range(S4 // 2))
                if e + 2 < E:
                    slot_spread(e + 2)
                layer2(e, range(S4 // 2, S4))


def shape_constants():
    p = np.arange(P)
    cf = np.zeros((P, NCF), np.float32)
    ch = np.zeros((P, NCH), np.float16)
    cf[:, slice(*CF["ident"])] = np.eye(P)
    cf[:, slice(*CF["sel"])] = p[:, None] == np.arange(E)[None]
    k = np.arange(KT)
    act = k >= KV
    sign = np.where(act, -1.0, 1.0)
    cf[:, slice(*CF["start"])] = -KEY_MID * sign
    cf[:, slice(*CF["need"])] = np.where(act, 2.0 * CAP - N, CAP)
    for r in range(ROUNDS):
        step = float(KT + 1) ** -(r + 1)
        cf[:, CF["step"][0] + r * KT:CF["step"][0] + (r + 1) * KT] = sign * step
        cf[:, CF["offset"][0] + r * KT:CF["offset"][0] + (r + 1) * KT] = sign * ((k + 1) * step - act * KEY_ULP / 2)
    cf[:, slice(*CF["octet"])] = np.arange(NA)[None] // S4 == p[:, None] % (P // NB)
    cf[:, slice(*CF["spare"])] = N + p[:, None] * S4 + np.arange(S4)[None]
    ch[:, slice(*CH["tok"])] = np.arange(NT)[None] * P + p[:, None] - N // 2
    ch[:, slice(*CH["iota"])] = np.arange(NA)[None]
    b_of_p = p // (P // NB)
    spread = np.zeros((P, P))
    for b in range(NB):
        spread[b] = b_of_p == b
        spread[NB + b] = (b_of_p == b) * FILLED
    ch[:, slice(*CH["spread"])] = spread
    ch[:, slice(*CH["ones"])] = 1
    ch[:, slice(*CH["chunks"])] = p[:, None] % E == p[None] % E
    ch[:, slice(*CH["lower"])] = p[:, None] < p[None]
    return cf, ch


def kernel(x, cond_256, L0_cond_q_right, L0_cond_spectral_gate, L0_ffn_gate_w, L0_ffn_w1, L0_ffn_w2):
    import concourse.bacc as bacc
    from concourse.bass_utils import run_bass_kernel_spmd

    rows = np.ascontiguousarray(np.asarray(x).reshape(N, D))
    xt = np.ascontiguousarray(rows.reshape(NG, TG, C4, P).transpose(0, 3, 2, 1))
    gw = np.asarray(L0_ffn_gate_w).reshape(E, C4, P).transpose(2, 1, 0).reshape(P, C4 * E)
    small = np.ascontiguousarray(np.concatenate(
        [np.asarray(cond_256).T, np.asarray(L0_cond_q_right).T, np.asarray(L0_cond_spectral_gate).reshape(P, 1), gw], axis=1))
    w1 = np.ascontiguousarray(np.asarray(L0_ffn_w1).reshape(E, F, C4, P).transpose(0, 3, 2, 1))
    w2 = np.ascontiguousarray(np.asarray(L0_ffn_w2).reshape(E, D, F4, P).transpose(0, 3, 2, 1))
    cf, ch = shape_constants()

    nc = bacc.Bacc("TRN2", target_bir_lowering=False, num_devices=1)
    arrays, aps = {}, []
    for name, a in (("xt", xt), ("x", rows), ("small", small), ("w1", w1), ("w2", w2), ("cf", cf), ("ch", ch)):
        arrays[f"in_{name}"] = a
        aps.append(nc.dram_tensor(f"in_{name}", a.shape, mybir.dt.from_np(a.dtype), kind="ExternalInput").ap())
    out = nc.dram_tensor("out", (N + SPARE, D), FP32, kind="ExternalOutput").ap()
    build(nc, *aps, out)
    r = run_bass_kernel_spmd(nc, [arrays], core_ids=[0])
    return np.asarray(r.results[0]["out"])[0:N].reshape(B, T_SEQ, D)
```

```python
import numpy as np
from contextlib import ExitStack

import concourse.bass as bass
from concourse import mybir

FP32 = mybir.dt.float32
F32R = mybir.dt.float32r
FP16 = mybir.dt.float16
U32 = mybir.dt.uint32
I32 = mybir.dt.int32
ALU = mybir.AluOpType
ACT = mybir.ActivationFunctionType
AX = mybir.AxisListType

P = 128
B, T_SEQ, D = 8, 512, 512
N = B * T_SEQ
NT = N // P
E, F = 8, 512
CAP = N // E
C4 = D // P
F4 = F // P
S4 = CAP // P
TG = 512
NG = N // TG
TPG = TG // P
CHUNKS = ((0, 12), (12, 24), (24, 32))
GW = 32
XRING = 4
KV, KA = 4, 3
KT = KV + KA
ROUNDS = 8
TC = P // E
KEY_MID = 0.5
NA, NB = 32, 16
SPARE = CAP
NEPS = 1e-8
THRESHOLD = 0.9
KEY_ULP = 2.0 ** -24
FILLED = -6144.0
EMPTY = 8192.0
CF, NCF = {}, 0
for _name, _width in (("ident", P), ("sel", E), ("ranks", E), ("signA", 16), ("signB", 16), ("octet", NA), ("spare", S4), ("start", KT), ("need", KT),
                      ("step", ROUNDS * KT), ("offset", ROUNDS * KT)):
    CF[_name] = (NCF, NCF + _width)
    NCF += _width
CH, NCH = {}, 0
for _name, _width in (("tok", NT), ("iota", NA * NT), ("spread", P), ("ones", P), ("chunks", P), ("lower", P)):
    CH[_name] = (NCH, NCH + _width)
    NCH += _width
QA, QB, QG = 13, 29, 45
NQ = QG + E * C4

SA = [[1, -1, -1, -1], [1, 1, -1, 1], [1, 1, 1, -1], [1, -1, 1, 1]]
SB = [[1, 1, 1, 1], [-1, 1, -1, 1], [-1, 1, 1, -1], [-1, -1, 1, 1]]


def build(nc, xt_d, x_d, small_d, w1_d, w2_d, cf_d, ch_d, out_d):
    probs_d = nc.dram_tensor("probs_scratch", (N * E, 1), FP32, kind="Internal").ap()
    ctx = ExitStack()
    with ctx:
        ctx.enter_context(nc.allow_low_precision(reason="counts up to 256 are exact in float16"))

        def sb(name, shape, dt=FP32):
            return ctx.enter_context(nc.sbuf_tensor(name, shape, dt))

        def sem(name):
            return ctx.enter_context(nc.semaphore(name))

        cf = sb("cf", [P, NCF])
        ch = sb("ch", [P, NCH], FP16)
        small = sb("small", [P, NQ])
        cfv = lambda k: cf[:, CF[k][0]:CF[k][1]]
        chv = lambda k: ch[:, CH[k][0]:CH[k][1]]

        sq = sb("sq", [P, 12])
        nrm = sb("nrm", [P, 12])
        facA = sb("facA", [P, 4, 4])
        facB = sb("facB", [P, 4, 4])
        ham = sb("ham", [P, 4, 4, 4])
        rot = sb("rot", [P, 4, 4])
        gprod = sb("gprod", [P, C4, E, C4])
        gfold = sb("gfold", [P, C4, GW])

        region = sb("region", [P, XRING * C4 * TG])
        xt = region[:, :].rearrange("p (r c n) -> p r c n", r=XRING, c=C4)
        lev = sb("lev", [P, NT, E, E], FP16)
        tk = lambda name: sb(name, [P, NT, E])
        cent, prob, rank, csum, arank, key, ulp = (tk(n) for n in ("cent", "prob", "rank", "csum", "arank", "key", "ulp"))
        rmax = sb("rmax", [P, NT])
        rsum = sb("rsum", [P, NT])
        lowlev = sb("lowlev", [P, E, E])
        rstar = sb("rstar", [P, E])
        keys = sb("keys", [P, N // TC])
        hits = region[:, 0:KT * N // TC // 2].bitcast(FP16).rearrange("p (k n) -> p k n", k=KT)
        base = sb("base", [P, 2, KT])
        thr = sb("thr", [P, 2, KT])
        nxt = sb("nxt", [P, KT])
        cnt = sb("cnt", [P, 2, KT], FP16)
        passed = sb("passed", [P, KT])
        best = sb("best", [P, 1])
        tb = sb("tb", [P, E])
        mask = sb("mask", [P, E, 2, NT], FP16)
        seg = sb("seg", [P, E * 2 * NT], FP16)
        incl = sb("incl", [P, E, 2, NT], FP16)
        off = sb("off", [P, E, 2])
        places = region[:, N // 2:N].rearrange("p (q e t) -> p q e t", e=E, t=NT)
        pos = places[:, 0:2].rearrange("p q e t -> p (q e t)").rearrange("p (e m t) -> p e m t", m=2, t=NT)
        posi = places[:, 2].bitcast(I32)
        pab = places[:, 3:5].bitcast(I32).rearrange("p q e t -> p (q e t)").rearrange("p (e m t) -> p e m t", m=2, t=NT)
        ab = sb("ab", [P, E, 2, NT], FP16)
        hotA = sb("hotA", [P, NA, NT], FP16)
        hotB = sb("hotB", [P, 2 * NB, NT], FP16)
        tabU = sb("tabU", [2 * NB, NA], FP16)
        tabV = sb("tabV", [P, NA])
        tabf = sb("tabf", [P, S4])
        scat = sb("scat", [P, E, S4], U32)
        gath = sb("gath", [P, E, S4], U32)
        pidx = sb("pidx", [P, E, S4], U32)

        w1raw = sb("w1raw", [P, 2, C4, F])
        w2raw = sb("w2raw", [P, F4, D])
        w1rot = sb("w1rot", [P, C4, F])
        w1h = [sb(f"w1h{i}", [P, C4, F], F32R) for i in range(2)]
        w1l = [sb(f"w1l{i}", [P, C4, F], F32R) for i in range(2)]
        w2h = [sb(f"w2h{i}", [P, F4, D], F32R) for i in range(2)]
        w2l = [sb(f"w2l{i}", [P, F4, D], F32R) for i in range(2)]
        xg = sb("xg", [P, S4, D])
        xh = sb("xh", [P, C4, CAP], F32R)
        xl = sb("xl", [P, C4, CAP], F32R)
        hf = sb("hf", [P, 2, CAP])
        hh = sb("hh", [P, F4, CAP], F32R)
        hl = sb("hl", [P, F4, CAP], F32R)
        score = sb("score", [P, 2, S4])
        ysb = sb("ysb", [P, S4, D])
        warm = sb("warm", [P, 1])
        before = xg[:, 0:2, :].rearrange("p s d -> p (s d)").rearrange("p (t e f) -> p t e f", e=E, f=E)
        mass = xg[:, 2:4, :].rearrange("p s d -> p (s d)").rearrange("p (t e f) -> p t e f", e=E, f=E)
        parts = hf[:, :, 0:P]
        diag = ysb[:, :, :].rearrange("p s d -> p (s d)").rearrange("p (q c) -> p q c", c=P)

        bank = [ctx.enter_context(nc.psum_tensor(f"bank{i}", [P, 512], FP32)) for i in range(8)]
        xbank, hbank, ybank = bank[0:2], bank[2:4], bank[4:6]
        ubank, vbank = bank[6], bank[7]
        xb = lambda e, j: bank[(0, 1, 4, 5)[j]] if e == 0 else xbank[j % 2]
        pbank, lbank, rbank = bank[1:3], [bank[i] for i in (0, 3, 5)], bank[4]
        fbank, kbank, cbank, obank = [bank[i] for i in (6, 0, 3, 5)], bank[7], bank[1:3], bank[3]

        small_in, cf_in, ch_in = sem("small_in"), sem("cf_in"), sem("ch_in")
        xt_in = [sem(f"xt_in{i}") for i in range(XRING)]
        w1_in = [sem(f"w1_in{i}") for i in range(2)]
        w2_in = sem("w2_in")
        out_base, probs_out = sem("out_base"), sem("probs_out")
        squares, roots = sem("squares"), sem("roots")
        rot_ready, diag_ready, fold_mm = sem("rot_ready"), sem("diag_ready"), sem("fold_mm")
        gate_folded, parts_mm, parts_ev, logits_mm = sem("gate_folded"), sem("parts_mm"), sem("parts_ev"), sem("logits_mm")
        dve_step = sem("dve_step")
        centred, exped, prob_ready = sem("centred"), sem("exped"), sem("prob_ready")
        lev_ready, lev_mm = sem("lev_ready"), sem("lev_mm")
        key_ready, key_mm = sem("key_ready"), sem("key_mm")
        thr_ready, cnt_v, cnt_a, cnt_mm = sem("thr_ready"), sem("cnt_v"), sem("cnt_a"), sem("cnt_mm")
        base_ready, tb_mm = sem("base_ready"), sem("tb_mm")
        incl_ready, off_mm = sem("incl_ready"), sem("off_mm")
        hot_ready, u_mm, u_ev, v_mm, slots_ready = (sem(n) for n in ("hot_ready", "u_mm", "u_ev", "v_mm", "slots_ready"))
        xg_in = [sem(f"xg_in{i}") for i in range(S4)]
        score_in = [sem(f"score_in{i}") for i in range(2)]
        xt_mm, x_hi, x_lo = sem("xt_mm"), sem("x_hi"), sem("x_lo")
        w1_rot, w1_hi, w1_lo = sem("w1_rot"), sem("w1_hi"), sem("w1_lo")
        w2_hi, w2_lo = sem("w2_hi"), sem("w2_lo")
        h_mm, h_act, h_hi, h_lo = sem("h_mm"), sem("h_act"), sem("h_hi"), sem("h_lo")
        y_mm, y_ev = sem("y_mm"), sem("y_ev")
        added = [sem(f"added{i}") for i in range(S4)]

        block = ctx.enter_context(nc.Block())

        @block.sync
        def _(sp):
            sp.dma_start(small[:, :], small_d).then_inc(small_in, 16)

            def load_x(g):
                if g >= XRING:
                    sp.wait_ge(parts_mm, g - XRING + 1)
                sp.dma_start(xt[:, g % XRING], xt_d[g]).then_inc(xt_in[g % XRING], 16)

            def load_w1(e):
                if e >= 2:
                    sp.wait_ge(w1_rot, C4 * (e - 1))
                sp.dma_start(w1raw[:, e % 2], w1_d[e]).then_inc(w1_in[e % 2], 16)

            def load_w2(e):
                if e >= 1:
                    sp.wait_ge(w2_lo, e)
                sp.dma_start(w2raw[:, :, :], w2_d[e]).then_inc(w2_in, 16)

            sp.dma_start(cf[:, :], cf_d).then_inc(cf_in, 16)
            for g in range(NG // 2):
                load_x(g)
            sp.dma_start(ch[:, :], ch_d).then_inc(ch_in, 16)
            for g in range(NG // 2, NG):
                load_x(g)
            load_w1(0)
            load_w1(1)
            load_w2(0)
            sp.dma_start(out_d[0:N, :], x_d).then_inc(out_base, 16)
            sp.dma_start(out_d[N:N + SPARE, :], x_d[0:SPARE, :]).then_inc(out_base, 16)
            sp.wait_ge(prob_ready, len(CHUNKS))
            sp.dma_start(probs_d.rearrange("(p n) o -> p (n o)", p=P),
                         prob[:, :, :].rearrange("p t e -> p (t e)")).then_inc(probs_out, 16)
            for e in range(1, E):
                load_w2(e)
                if e + 1 < E:
                    load_w1(e + 1)
            for s in range(S4):
                sp.wait_ge(added[s], 16 * E)

        @block.gpsimd
        def _(pool):
            def gather(e):
                pool.wait_ge(slots_ready, e + 1)
                if e >= 1:
                    pool.wait_ge(xt_mm, C4 * e)
                for s in range(S4):
                    pool.indirect_dma_start(xg[:, s, :], None, x_d,
                                            bass.IndirectOffsetOnAxis(gath[:, e, s:s + 1], 0)).then_inc(xg_in[s], 16)
                for s in range(S4):
                    pool.indirect_dma_start(score[:, e % 2, s:s + 1], None, probs_d,
                                            bass.IndirectOffsetOnAxis(pidx[:, e, s:s + 1], 0)).then_inc(score_in[e % 2], 16)

            def scatter(e):
                for s in range(S4):
                    if e >= 1:
                        pool.wait_ge(added[s], 16 * e)
                for s in range(S4):
                    pool.wait_ge(y_ev, S4 * e + s + 1)
                    pool.indirect_dma_start(out_d, bass.IndirectOffsetOnAxis(scat[:, e, s:s + 1], 0),
                                            ysb[:, s, :], None, compute_op=ALU.add).then_inc(added[s], 16)

            pool.wait_ge(probs_out, 16)
            gather(0)
            for e in range(E):
                if e + 1 < E:
                    gather(e + 1)
                if e == 0:
                    pool.wait_ge(out_base, 32)
                scatter(e)

        @block.scalar
        def _(act):
            act.wait_ge(squares, 1)
            nc.scalar.activation(nrm[:, 4:6], nrm[:, 2:4], ACT.Sqrt).then_inc(roots, 1)

            def w1_high(e, j):
                act.wait_ge(w1_rot, C4 * e + j + 1)
                if e >= 2:
                    act.wait_ge(h_mm, F4 * (e - 1))
                nc.scalar.activation(w1h[e % 2][:, j, :], w1rot[:, j, :], ACT.Copy).then_inc(w1_hi, 1)

            def w2_high(e):
                act.wait_ge(w2_in, 16 * (e + 1))
                if e >= 2:
                    act.wait_ge(y_mm, S4 * (e - 1))
                nc.scalar.activation(w2h[e % 2][:, :, :], w2raw[:, :, :], ACT.Copy).then_inc(w2_hi, 1)

            def x_high(e, j):
                act.wait_ge(xt_mm, C4 * e + j + 1)
                nc.scalar.activation(xh[:, j, :], xb(e, j)[:, :], ACT.Copy).then_inc(x_hi, 1)

            def hidden(e, f):
                n = F4 * e + f
                act.wait_ge(h_mm, n + 1)
                if n >= 2:
                    act.wait_ge(h_lo, n - 1)
                nc.scalar.activation(hf[:, n % 2, :], hbank[n % 2][:, :], ACT.Gelu).then_inc(h_act, 1)
                act.wait_ge(h_act, n + 1)
                if e >= 1:
                    act.wait_ge(y_mm, S4 * e)
                nc.scalar.activation(hh[:, f, :], hf[:, n % 2, :], ACT.Copy).then_inc(h_hi, 1)

            def y_out(e, s):
                n = S4 * e + s
                act.wait_ge(y_mm, n + 1)
                if s == 0:
                    act.wait_ge(score_in[e % 2], 16 * S4 * (e // 2 + 1))
                if e >= 1:
                    act.wait_ge(added[s], 16 * e)
                nc.scalar.activation(ysb[:, s, :], ybank[n % 2][:, :], ACT.Copy,
                                     scale=score[:, e % 2, s:s + 1]).then_inc(y_ev, 1)

            act.wait_ge(rot_ready, 1)
            for q in range(16):
                last = nc.scalar.activation(diag[:, q, :], cfv("ident"), ACT.Copy,
                                            scale=rot[:, q // 4, q % 4:q % 4 + 1])
            last.then_inc(diag_ready, 1)

            def part_out(g):
                act.wait_ge(parts_mm, g + 1)
                if g >= 2:
                    act.wait_ge(logits_mm, g - 1)
                nc.scalar.activation(parts[:, g % 2, :], pbank[g % 2][:, 0:P], ACT.Copy).then_inc(parts_ev, 1)

            def exp(c):
                lo, hi = CHUNKS[c]
                act.wait_ge(centred, c + 1)
                nc.scalar.activation(cent[:, lo:hi], cent[:, lo:hi], ACT.Exp).then_inc(exped, 1)

            def w1_folded(j):
                act.wait_ge(fold_mm, j + 1)
                nc.scalar.activation(w1rot[:, j, :], fbank[j][:, :], ACT.Copy).then_inc(w1_rot, 1)

            g = 0
            for c, (_, hi) in enumerate(CHUNKS):
                while g < min(hi // TPG + 1, NG):
                    part_out(g)
                    g += 1
                exp(c)
            w1_folded(0)
            w1_high(0, 0)
            w1_folded(1)
            w1_high(0, 1)
            for r in range(ROUNDS):
                act.wait_ge(thr_ready, r + 1)
                if r >= 2:
                    act.wait_ge(cnt_mm, r - 1)
                for k in range(KV, KT):
                    last = nc.scalar.activation(hits[:, k, :], keys[:, :], ACT.Sign, bias=thr[:, r % 2, k:k + 1],
                                                accum_out=cnt[:, r % 2, k:k + 1])
                last.then_inc(cnt_a, 1)
                if r == ROUNDS // 2 + 1:
                    w1_folded(2)
                    w1_high(0, 2)
            w1_folded(3)
            w1_high(0, 3)
            w2_high(0)
            nc.scalar.activation(warm[:, :], cfv("ident")[:, 0:1], ACT.Gelu)
            for j in range(C4):
                x_high(0, j)
            for e in range(E):
                more = e + 1 < E
                hidden(e, 0)
                hidden(e, 1)
                if more:
                    w1_high(e + 1, 0)
                hidden(e, 2)
                if more:
                    w1_high(e + 1, 1)
                hidden(e, 3)
                if more:
                    x_high(e + 1, 0)
                    x_high(e + 1, 1)
                    w1_high(e + 1, 2)
                y_out(e, 0)
                if more:
                    x_high(e + 1, 2)
                    x_high(e + 1, 3)
                    w1_high(e + 1, 3)
                y_out(e, 1)
                if more:
                    w2_high(e + 1)
                y_out(e, 2)
                y_out(e, 3)

        @block.vector
        def _(dve):
            steps = [0]

            def then(ins):
                steps[0] += 1
                ins.then_inc(dve_step, 1)
                dve.wait_ge(dve_step, steps[0])

            def rotate_w1(e, j):
                if j == 0:
                    dve.wait_ge(w1_in[e % 2], 16 * (e // 2 + 1))
                    if e >= 1:
                        dve.wait_ge(w1_lo, e)
                dst = w1rot[:, j, :]
                then(nc.vector.tensor_scalar(dst, w1raw[:, e % 2, 0, :], rot[:, j, 0:1], None, ALU.mult))
                for i in range(1, C4):
                    ins = nc.vector.scalar_tensor_tensor(dst, w1raw[:, e % 2, i, :], rot[:, j, i:i + 1], dst,
                                                         ALU.mult, ALU.add)
                    if i < C4 - 1:
                        then(ins)
                ins.then_inc(w1_rot, 1)

            def w1_low(e):
                dve.wait_ge(w1_hi, C4 * (e + 1))
                nc.vector.tensor_tensor(w1l[e % 2][:, :, :], w1rot[:, :, :], w1h[e % 2][:, :, :].bitcast(FP32),
                                        ALU.subtract).then_inc(w1_lo, 1)

            def w2_low(e):
                dve.wait_ge(w2_hi, e + 1)
                nc.vector.tensor_tensor(w2l[e % 2][:, :, :], w2raw[:, :, :], w2h[e % 2][:, :, :].bitcast(FP32),
                                        ALU.subtract).then_inc(w2_lo, 1)

            def x_low(e, j):
                dve.wait_ge(x_hi, C4 * e + j + 1)
                nc.vector.tensor_tensor(xl[:, j, :], xb(e, j)[:, :], xh[:, j, :].bitcast(FP32),
                                        ALU.subtract).then_inc(x_lo, 1)

            def h_low(e, f):
                n = F4 * e + f
                dve.wait_ge(h_hi, n + 1)
                nc.vector.tensor_tensor(hl[:, f, :], hf[:, n % 2, :], hh[:, f, :].bitcast(FP32),
                                        ALU.subtract).then_inc(h_lo, 1)

            def one_hots(e):
                if e >= 1:
                    dve.wait_ge(u_mm, e)
                iota = chv("iota").rearrange("p (a t) -> p a t", t=NT)
                nc.vector.tensor_tensor(hotA[:, :, :], ab[:, e, 0, :].unsqueeze(1).to_broadcast([P, NA, NT]),
                                        iota, ALU.is_equal)
                then(nc.vector.tensor_tensor(hotB[:, NB:, :], ab[:, e, 1, :].unsqueeze(1).to_broadcast([P, NB, NT]),
                                             iota[:, 0:NB, :], ALU.is_equal))
                nc.vector.tensor_tensor(hotB[:, 0:NB, :], hotB[:, NB:, :],
                                        chv("tok").unsqueeze(1).to_broadcast([P, NB, NT]), ALU.mult).then_inc(hot_ready, 1)

            def table_rows(e):
                dve.wait_ge(u_mm, e + 1)
                nc.vector.tensor_copy(tabU[:, :], ubank[0:2 * NB, 0:NA]).then_inc(u_ev, 1)

            def slot_tables(e):
                dve.wait_ge(v_mm, e + 1)
                then(nc.vector.tensor_tensor(tabV[:, :], vbank[:, 0:NA], cfv("octet"), ALU.mult))
                then(nc.vector.tensor_reduce(tabf[:, :], tabV[:, :].rearrange("p (g c) -> p c g", c=S4), AX.X, ALU.add))
                nc.vector.scalar_tensor_tensor(scat[:, e, :], tabf[:, :], EMPTY, cfv("spare"), ALU.add, ALU.min)
                then(nc.vector.tensor_scalar(tabV[:, 0:S4], tabf[:, :], EMPTY, float(N - 1), ALU.add, ALU.min))
                nc.vector.tensor_scalar(pidx[:, e, :], tabV[:, 0:S4], float(E), float(e), ALU.mult, ALU.add)
                nc.vector.tensor_copy(gath[:, e, :], tabV[:, 0:S4]).then_inc(slots_ready, 1)

            def places(e0, e1):
                w = e1 - e0
                flat = lambda x: x[:, e0:e1].rearrange("p e m t -> p (e m t)")
                for m, op in enumerate((ALU.is_gt, ALU.is_equal)):
                    ins = nc.vector.tensor_tensor(mask[:, e0:e1, m, :].rearrange("p e t -> p t e"), key[:, :, e0:e1],
                                                  tb[:, e0:e1].unsqueeze(1).to_broadcast([P, NT, w]), op)
                then(ins)
                nc.vector.tensor_tensor_scan(flat(incl), seg[:, 0:w * 2 * NT], flat(mask), 0.0, ALU.mult,
                                             ALU.add).then_inc(incl_ready, 1)
                dve.wait_ge(off_mm, 1 if e0 == 0 else 2)
                low = obank[:, 0:2 * w].rearrange("p (e m) -> p e m", m=2)
                tot = obank[:, 2 * w:4 * w].rearrange("p (e m) -> p e m", m=2)
                then(nc.vector.tensor_scalar(off[:, e0:e1, :], low, 1.0 + 2 * N, None, ALU.subtract))
                then(nc.vector.tensor_tensor(off[:, e0:e1, 1:2], off[:, e0:e1, 1:2], tot[:, :, 0:1], ALU.add))
                then(nc.vector.tensor_tensor(pos[:, e0:e1], incl[:, e0:e1],
                                             off[:, e0:e1, :].unsqueeze(3).to_broadcast([P, w, 2, NT]), ALU.add))
                then(nc.vector.tensor_tensor(flat(pos), flat(pos), flat(mask), ALU.mult))
                then(nc.vector.scalar_tensor_tensor(posi[:, e0:e1], pos[:, e0:e1, 0, :], 2.0 * N, pos[:, e0:e1, 1, :],
                                                    ALU.add, ALU.add))
                nc.vector.tensor_scalar(pab[:, e0:e1, 0, :], posi[:, e0:e1], 4, None, ALU.logical_shift_right)
                then(nc.vector.tensor_scalar(pab[:, e0:e1, 1, :], posi[:, e0:e1], NB - 1, None, ALU.bitwise_and))
                then(nc.vector.tensor_copy(flat(ab), flat(pab)))

            nc.vector.memset(gfold[:, :, :], 0.0)
            dve.wait_ge(small_in, 16)
            then(nc.vector.tensor_tensor(sq[:, :], small[:, 0:12], small[:, 0:12], ALU.mult))
            nc.vector.tensor_reduce(nrm[:, 0:1], sq[:, 0:8], AX.X, ALU.add)
            then(nc.vector.tensor_reduce(nrm[:, 1:2], sq[:, 8:12], AX.X, ALU.add))
            nc.vector.tensor_scalar(nrm[:, 2:4], nrm[:, 0:2], NEPS, None, ALU.add).then_inc(squares, 1)
            dve.wait_ge(cf_in, 16)
            nc.vector.tensor_tensor(facA[:, :, :].rearrange("p i k -> p (i k)"), small[:, QA:QB], cfv("signA"), ALU.mult)
            then(nc.vector.tensor_tensor(facB[:, :, :].rearrange("p j k -> p (j k)"), small[:, QB:QG], cfv("signB"), ALU.mult))
            then(nc.vector.tensor_tensor(ham[:, :, :, :], facA[:, :, :].unsqueeze(1).to_broadcast([P, 4, 4, 4]),
                                         facB[:, :, :].unsqueeze(2).to_broadcast([P, 4, 4, 4]), ALU.mult))
            nc.vector.tensor_reduce(rot[:, :, :], ham[:, :, :, :], AX.X, ALU.add)
            dve.wait_ge(roots, 1)
            then(nc.vector.reciprocal(nrm[:, 6:8], nrm[:, 4:6]))
            then(nc.vector.tensor_tensor(nrm[:, 6:8], nrm[:, 6:8], nrm[:, 2:4], ALU.mult))
            then(nc.vector.tensor_tensor(nrm[:, 6:8], nrm[:, 6:8], nrm[:, 4:6], ALU.add))
            then(nc.vector.tensor_tensor(nrm[:, 8:9], nrm[:, 6:7], nrm[:, 7:8], ALU.mult))
            then(nc.vector.reciprocal(nrm[:, 9:10], nrm[:, 8:9]))
            then(nc.vector.tensor_scalar(nrm[:, 10:11], nrm[:, 9:10], small[:, 12:13], 4.0, ALU.mult, ALU.mult))
            nc.vector.tensor_scalar(rot[:, :, :], rot[:, :, :], nrm[:, 10:11], None, ALU.mult).then_inc(rot_ready, 1)
            dve.wait_ge(rot_ready, 1)
            gw = small[:, QG:NQ].rearrange("p (e c) -> p e c", c=C4)
            then(nc.vector.tensor_tensor(gprod[:, :, :, :], rot[:, :, :].unsqueeze(2).to_broadcast([P, C4, E, C4]),
                                         gw.unsqueeze(1).to_broadcast([P, C4, E, C4]), ALU.mult))
            nc.vector.tensor_reduce(gfold[:, :, 0:E], gprod[:, :, :, :], AX.X, ALU.add).then_inc(gate_folded, 1)
            nc.vector.memset(seg[:, :], 1.0)
            then(nc.vector.memset(before, 0.0))
            nc.vector.memset(seg[:, :].rearrange("p (g t) -> p g t", t=NT)[:, :, 0:1], 0.0)

            def route(c):
                lo, hi = CHUNKS[c]
                w = hi - lo
                sl = slice(lo, hi)
                logits = lbank[c][:, 0:w * GW].rearrange("p (t x) -> p t x", x=GW)[:, :, 0:E]
                bef, mas = before[:, 0:w], mass[:, 0:w]
                wide = lambda a: a.unsqueeze(2).to_broadcast([P, w, E])
                dve.wait_ge(logits_mm, hi // TPG)
                then(nc.vector.tensor_reduce(rmax[:, sl], logits, AX.X, ALU.max))
                nc.vector.tensor_tensor(cent[:, sl], logits, wide(rmax[:, sl]), ALU.subtract).then_inc(centred, 1)
                dve.wait_ge(exped, c + 1)
                then(nc.vector.tensor_reduce(rsum[:, sl], cent[:, sl], AX.X, ALU.add))
                then(nc.vector.reciprocal(rsum[:, sl], rsum[:, sl]))
                nc.vector.tensor_tensor(prob[:, sl], cent[:, sl], wide(rsum[:, sl]), ALU.mult).then_inc(prob_ready, 1)
                dve.wait_ge(prob_ready, c + 1)
                for e in range(E):
                    for f0, f1, op in ((0, e, ALU.is_ge), (e + 1, E, ALU.is_gt)):
                        if f0 < f1:
                            last = nc.vector.tensor_tensor(bef[:, :, e, f0:f1], prob[:, sl, f0:f1],
                                                           prob[:, sl, e:e + 1].to_broadcast([P, w, f1 - f0]), op)
                then(last)
                nc.vector.tensor_reduce(rank[:, sl], bef, AX.X, ALU.add)
                then(nc.vector.tensor_tensor(mas, bef, prob[:, sl].unsqueeze(2).to_broadcast([P, w, E, E]), ALU.mult))
                nc.vector.tensor_reduce(csum[:, sl], mas, AX.X, ALU.add)
                then(nc.vector.tensor_scalar(rank[:, sl], rank[:, sl], 1.0, None, ALU.add))
                nc.vector.tensor_scalar(csum[:, sl], csum[:, sl], THRESHOLD, 16.0, ALU.is_ge, ALU.mult)
                then(nc.vector.tensor_tensor(key[:, sl], prob[:, sl], rank[:, sl], ALU.subtract))
                nc.vector.tensor_tensor(arank[:, sl], rank[:, sl], csum[:, sl], ALU.add)
                nc.vector.tensor_scalar(ulp[:, sl], rank[:, sl], 1.0, KEY_ULP, ALU.is_equal, ALU.mult)
                then(nc.vector.tensor_tensor(key[:, sl], key[:, sl], rank[:, sl], ALU.add))
                nc.vector.tensor_tensor(lev[:, sl], arank[:, sl].unsqueeze(2).to_broadcast([P, w, E, E]),
                                        cfv("ranks").unsqueeze(1).unsqueeze(3).to_broadcast([P, w, E, E]),
                                        ALU.is_le).then_inc(lev_ready, 1)
                then(nc.vector.scalar_tensor_tensor(key[:, sl], key[:, sl], KEY_MID, ulp[:, sl], ALU.subtract, ALU.subtract))

            for c in range(len(CHUNKS)):
                route(c)
            dve.wait_ge(lev_mm, 1)
            then(nc.vector.tensor_scalar(lowlev[:, :, :], rbank[:, 0:E * E].rearrange("p (r e) -> p e r", e=E),
                                         float(CAP), None, ALU.is_lt))
            then(nc.vector.tensor_reduce(rstar[:, :], lowlev[:, :, :], AX.X, ALU.add))
            then(nc.vector.scalar_tensor_tensor(arank[:, :, :], rstar[:, :].unsqueeze(1).to_broadcast([P, NT, E]), 1.0,
                                                arank[:, :, :], ALU.add, ALU.subtract))
            then(nc.vector.scalar_tensor_tensor(key[:, :, :], arank[:, :, :], 4.0, key[:, :, :], ALU.mult, ALU.add))
            nc.vector.tensor_scalar(key[:, :, :], key[:, :, :], 2.0, -1.0, ALU.min, ALU.max).then_inc(key_ready, 1)
            table = lambda k, r: cfv(k)[:, r * KT:(r + 1) * KT]
            nc.vector.tensor_copy(base[:, 0, :], cfv("start"))
            dve.wait_ge(key_mm, 1)
            nc.vector.tensor_copy(keys[:, :], kbank[:, 0:N // TC])
            nc.vector.tensor_tensor(thr[:, 0, :], cfv("start"), table("offset", 0), ALU.add).then_inc(thr_ready, 1)
            dve.wait_ge(thr_ready, 1)

            for r in range(ROUNDS):
                now, new = r % 2, (r + 1) % 2
                if r + 1 < ROUNDS:
                    nc.vector.tensor_tensor(nxt[:, :], base[:, now, :], table("offset", r + 1), ALU.add)
                if r >= 2:
                    dve.wait_ge(cnt_mm, r - 1)
                for k in range(KV):
                    last = nc.vector.tensor_scalar(hits[:, k, :], keys[:, :], thr[:, now, k:k + 1], None, ALU.is_ge, ALU.add,
                                                   accum_out=cnt[:, now, k:k + 1])
                last.then_inc(cnt_v, 1)
                dve.wait_ge(cnt_mm, r + 1)
                then(nc.vector.scalar_tensor_tensor(passed[:, :], cbank[now][:, 0:KT], 0.0, cfv("need"), ALU.add,
                                                    ALU.is_ge, accum_out=best[:, :]))
                if r + 1 < ROUNDS:
                    nc.vector.scalar_tensor_tensor(thr[:, new, :], table("step", r), best[:, :], nxt[:, :], ALU.mult,
                                                   ALU.add).then_inc(thr_ready, 1)
                ins = nc.vector.scalar_tensor_tensor(base[:, new, :], table("step", r), best[:, :], base[:, now, :],
                                                     ALU.mult, ALU.add)
                if r + 1 < ROUNDS:
                    then(ins)
            ins.then_inc(base_ready, 1)

            dve.wait_ge(tb_mm, 1)
            then(nc.vector.tensor_copy(tb[:, :], kbank[:, 0:E]))
            places(0, 1)
            one_hots(0)
            table_rows(0)
            slot_tables(0)
            w1_low(0)
            places(1, E)
            one_hots(1)
            for j in range(C4):
                x_low(0, j)

            for e in range(E):
                more = e + 1 < E
                w2_low(e)
                if 1 <= e < E - 2:
                    one_hots(e + 2)
                if e and more:
                    rotate_w1(e + 1, 0)
                h_low(e, 0)
                if e == 0:
                    table_rows(1)
                    rotate_w1(1, 0)
                if more:
                    rotate_w1(e + 1, 1)
                h_low(e, 1)
                if e == 0:
                    slot_tables(1)
                if more:
                    rotate_w1(e + 1, 2)
                h_low(e, 2)
                h_low(e, 3)
                if e == 0:
                    one_hots(2)
                if more:
                    x_low(e + 1, 0)
                    x_low(e + 1, 1)
                if e + 2 < E:
                    table_rows(e + 2)
                if more:
                    rotate_w1(e + 1, 3)
                    x_low(e + 1, 2)
                    x_low(e + 1, 3)
                    w1_low(e + 1)
                if e + 2 < E:
                    slot_tables(e + 2)

        @block.tensor
        def _(pe):
            ident = cfv("ident")

            def slot_rows(e):
                pe.wait_ge(hot_ready, e + 1)
                if e >= 1:
                    pe.wait_ge(u_ev, e)
                for t in range(NT):
                    last = nc.tensor.matmul(ubank[0:2 * NB, 0:NA], hotB[:, :, t], hotA[:, :, t],
                                            start=(t == 0), stop=(t == NT - 1))
                last.then_inc(u_mm, 1)

            def slot_spread(e):
                pe.wait_ge(u_ev, e + 1)
                if e >= 1:
                    pe.wait_ge(slots_ready, e)
                nc.tensor.matmul(vbank[:, 0:NA], chv("spread")[0:2 * NB, :], tabU[:, :],
                                 start=True, stop=True).then_inc(v_mm, 1)

            def transpose_x(e, chunks):
                for s in range(S4):
                    pe.wait_ge(xg_in[s], 16 * (e + 1))
                for j in chunks:
                    if e >= 1 and C4 * e + j >= C4 + 2:
                        pe.wait_ge(x_lo, C4 * e + j - 1)
                    elif e == 1:
                        pe.wait_ge(x_lo, C4)
                    for s in range(S4):
                        last = nc.tensor.transpose(xbank[j % 2][:, s * P:(s + 1) * P], xg[:, s, j * P:(j + 1) * P], ident)
                    last.then_inc(xt_mm, 1)

            def transpose_x0():
                for s in range(S4):
                    pe.wait_ge(xg_in[s], 16)
                    for j in range(C4):
                        last = nc.tensor.transpose(xb(0, j)[:, s * P:(s + 1) * P], xg[:, s, j * P:(j + 1) * P], ident)
                        if s == S4 - 1:
                            last.then_inc(xt_mm, 1)

            def split_product(dst, ah, al, bh, bl, first, last):
                nc.tensor.matmul(dst, ah, bh, start=first, stop=False)
                nc.tensor.matmul(dst, ah, bl, start=False, stop=False)
                return nc.tensor.matmul(dst, al, bh, start=False, stop=last)

            def layer1(e, f):
                if f == 0:
                    pe.wait_ge(w1_lo, e + 1)
                n = F4 * e + f
                if n >= 2:
                    pe.wait_ge(h_act, n - 1)
                fs = slice(f * P, (f + 1) * P)
                for j in range(C4):
                    if f == 0:
                        pe.wait_ge(x_lo, C4 * e + j + 1)
                    last = split_product(hbank[n % 2][:, :], w1h[e % 2][:, j, fs], w1l[e % 2][:, j, fs],
                                         xh[:, j, :], xl[:, j, :], j == 0, j == C4 - 1)
                last.then_inc(h_mm, 1)

            def layer2(e, s):
                if s == 0:
                    pe.wait_ge(w2_lo, e + 1)
                    pe.wait_ge(h_lo, F4 * (e + 1))
                n = S4 * e + s
                if n >= 2:
                    pe.wait_ge(y_ev, n - 1)
                ss = slice(s * P, (s + 1) * P)
                for f in range(F4):
                    last = split_product(ybank[n % 2][:, :], hh[:, f, ss], hl[:, f, ss],
                                         w2h[e % 2][:, f, :], w2l[e % 2][:, f, :], f == 0, f == F4 - 1)
                last.then_inc(y_mm, 1)

            def gate(g):
                pe.wait_ge(xt_in[g % XRING], 16 * (g // XRING + 1))
                if g >= 2:
                    pe.wait_ge(parts_ev, g - 1)
                for j in range(C4):
                    for u in range(TPG):
                        last = nc.tensor.matmul(pbank[g % 2][u * GW:(u + 1) * GW, 0:P], gfold[:, j, :],
                                                xt[:, g % XRING, j, u * P:(u + 1) * P], start=(j == 0), stop=(j == C4 - 1))
                last.then_inc(parts_mm, 1)

            def logits_by_token(g):
                pe.wait_ge(parts_ev, g + 1)
                c = next(c for c, (lo, hi) in enumerate(CHUNKS) if lo <= g * TPG < hi)
                at = g * TPG * GW - CHUNKS[c][0] * GW
                nc.tensor.transpose(lbank[c][:, at:at + P], parts[:, g % 2, :], ident).then_inc(logits_mm, 1)

            def count_ranks(c):
                pe.wait_ge(lev_ready, c + 1)
                for t in range(*CHUNKS[c]):
                    last = nc.tensor.matmul(rbank[:, 0:E * E], chv("ones"), lev[:, t].rearrange("p r e -> p (r e)"),
                                            start=(t == 0), stop=(t == NT - 1))
                if c == len(CHUNKS) - 1:
                    last.then_inc(lev_mm, 1)

            def fold(j, i):
                term = nc.tensor.matmul(fbank[j][:, :], diag[:, j * C4 + i, :], w1raw[:, 0, i, :],
                                        start=(i == 0), stop=(i == C4 - 1))
                if i == C4 - 1:
                    term.then_inc(fold_mm, 1)

            pe.wait_ge(gate_folded, 1)
            for g in range(NG):
                gate(g)
                if g == 0:
                    pe.wait_ge(cf_in, 16)
                else:
                    logits_by_token(g - 1)
            logits_by_token(NG - 1)
            pe.wait_ge(ch_in, 16)
            count_ranks(0)
            pe.wait_ge(diag_ready, 1)
            pe.wait_ge(w1_in[0], 16)
            for i in range(C4):
                fold(0, i)
            count_ranks(1)
            for i in range(C4):
                fold(1, i)
            count_ranks(2)
            pe.wait_ge(centred, len(CHUNKS))
            pe.wait_ge(cf_in, 16)
            pe.wait_ge(key_ready, 1)
            for c in range(NT // TC):
                last = nc.tensor.transpose(kbank[:, c * P:(c + 1) * P],
                                           key[:, c * TC:(c + 1) * TC, :].rearrange("p t e -> p (t e)"), ident)
            last.then_inc(key_mm, 1)
            for r in range(ROUNDS):
                fold(2 + r // C4, r % C4)
                pe.wait_ge(cnt_v, r + 1)
                pe.wait_ge(cnt_a, r + 1)
                nc.tensor.matmul(cbank[r % 2][:, 0:KT], chv("chunks"), cnt[:, r % 2, :],
                                 start=True, stop=True).then_inc(cnt_mm, 1)
            pe.wait_ge(base_ready, 1)
            nc.tensor.matmul(kbank[:, 0:E], base[:, ROUNDS % 2, 0:1].to_broadcast([P, P]), cfv("sel"),
                             start=True, stop=True).then_inc(tb_mm, 1)

            def count_before(n, e0, e1):
                pe.wait_ge(incl_ready, n + 1)
                ends = incl[:, e0:e1, :, NT - 1].rearrange("p e m -> p (e m)")
                w = 2 * (e1 - e0)
                nc.tensor.matmul(obank[:, 0:w], chv("lower"), ends, start=True, stop=True)
                nc.tensor.matmul(obank[:, w:2 * w], chv("ones"), ends, start=True, stop=True).then_inc(off_mm, 1)

            pe.wait_ge(w1_rot, C4)
            count_before(0, 0, 1)
            slot_rows(0)
            slot_spread(0)
            count_before(1, 1, E)
            transpose_x0()
            for e in range(E):
                layer1(e, 0)
                if e == 0:
                    slot_rows(1)
                layer1(e, 1)
                if e == 0:
                    slot_spread(1)
                layer1(e, 2)
                layer1(e, 3)
                if e + 1 < E:
                    transpose_x(e + 1, (0, 1))
                if e + 2 < E:
                    slot_rows(e + 2)
                layer2(e, 0)
                if e + 1 < E:
                    transpose_x(e + 1, (2, 3))
                layer2(e, 1)
                if e + 2 < E:
                    slot_spread(e + 2)
                layer2(e, 2)
                layer2(e, 3)


def shape_constants():
    p = np.arange(P)
    cf = np.zeros((P, NCF), np.float32)
    ch = np.zeros((P, NCH), np.float16)
    cf[:, slice(*CF["ident"])] = np.eye(P)
    cf[:, slice(*CF["sel"])] = p[:, None] == np.arange(E)[None]
    cf[:, slice(*CF["ranks"])] = np.arange(1, E + 1)[None]
    cf[:, slice(*CF["signA"])] = np.ravel(SA)[None]
    cf[:, slice(*CF["signB"])] = np.ravel(np.transpose(SB))[None]
    k = np.arange(KT)
    act = k >= KV
    sign = np.where(act, -1.0, 1.0)
    cf[:, slice(*CF["start"])] = -KEY_MID * sign
    cf[:, slice(*CF["need"])] = np.where(act, 2.0 * CAP - N, CAP)
    for r in range(ROUNDS):
        step = float(KT + 1) ** -(r + 1)
        cf[:, CF["step"][0] + r * KT:CF["step"][0] + (r + 1) * KT] = sign * step
        cf[:, CF["offset"][0] + r * KT:CF["offset"][0] + (r + 1) * KT] = sign * ((k + 1) * step - act * KEY_ULP / 2)
    cf[:, slice(*CF["octet"])] = np.arange(NA)[None] // S4 == p[:, None] % (P // NB)
    cf[:, slice(*CF["spare"])] = N + p[:, None] * S4 + np.arange(S4)[None]
    ch[:, slice(*CH["tok"])] = np.arange(NT)[None] + p[:, None] * NT - N // 2
    ch[:, slice(*CH["iota"])] = np.repeat(np.arange(NA), NT)[None]
    b_of_p = p // (P // NB)
    spread = np.zeros((P, P))
    for b in range(NB):
        spread[b] = b_of_p == b
        spread[NB + b] = (b_of_p == b) * FILLED
    ch[:, slice(*CH["spread"])] = spread
    ch[:, slice(*CH["ones"])] = 1
    ch[:, slice(*CH["chunks"])] = p[:, None] % E == p[None] % E
    ch[:, slice(*CH["lower"])] = p[:, None] < p[None]
    return cf, ch


def kernel(x, cond_256, L0_cond_q_right, L0_cond_spectral_gate, L0_ffn_gate_w, L0_ffn_w1, L0_ffn_w2):
    import concourse.bacc as bacc
    from concourse.bass_utils import run_bass_kernel_spmd

    rows = np.ascontiguousarray(np.asarray(x).reshape(N, D))
    xt = np.ascontiguousarray(rows.reshape(P, NG, TPG, C4, P).transpose(1, 4, 3, 2, 0)).reshape(NG, P, C4, TG)
    cond, right = np.asarray(cond_256).T, np.asarray(L0_cond_q_right).T
    xor = np.arange(4)[:, None] ^ np.arange(4)[None]
    gw = np.asarray(L0_ffn_gate_w).reshape(E, C4, P).transpose(2, 0, 1).reshape(P, E * C4)
    small = np.ascontiguousarray(np.concatenate(
        [cond, right, np.asarray(L0_cond_spectral_gate).reshape(P, 1), cond[:, xor.ravel()], right[:, xor.ravel()], gw], axis=1))
    w1 = np.ascontiguousarray(np.asarray(L0_ffn_w1).reshape(E, F, C4, P).transpose(0, 3, 2, 1))
    w2 = np.ascontiguousarray(np.asarray(L0_ffn_w2).reshape(E, D, F4, P).transpose(0, 3, 2, 1))
    cf, ch = shape_constants()

    nc = bacc.Bacc("TRN2", target_bir_lowering=False, num_devices=1)
    arrays, aps = {}, []
    for name, a in (("xt", xt), ("x", rows), ("small", small), ("w1", w1), ("w2", w2), ("cf", cf), ("ch", ch)):
        arrays[f"in_{name}"] = a
        aps.append(nc.dram_tensor(f"in_{name}", a.shape, mybir.dt.from_np(a.dtype), kind="ExternalInput").ap())
    out = nc.dram_tensor("out", (N + SPARE, D), FP32, kind="ExternalOutput").ap()
    build(nc, *aps, out)
    r = run_bass_kernel_spmd(nc, [arrays], core_ids=[0])
    return np.asarray(r.results[0]["out"])[0:N].reshape(B, T_SEQ, D)
```

```python
import numpy as np
from contextlib import ExitStack

import concourse.bass as bass
from concourse import mybir

FP32 = mybir.dt.float32
F32R = mybir.dt.float32r
FP16 = mybir.dt.float16
U32 = mybir.dt.uint32
I32 = mybir.dt.int32
ALU = mybir.AluOpType
ACT = mybir.ActivationFunctionType
AX = mybir.AxisListType

P = 128
B, T_SEQ, D = 8, 512, 512
N = B * T_SEQ
NT = N // P
E, F = 8, 512
CAP = N // E
C4 = D // P
F4 = F // P
S4 = CAP // P
TG = 512
NG = N // TG
TPG = TG // P
CHUNKS = ((0, 8), (8, 16), (16, 24), (24, 32))
GW = 32
XRING = 4
KV, KA = 4, 3
KT = KV + KA
ROUNDS = 8
TC = P // E
KEY_MID = 0.5
NA, NB = 32, 16
SPARE = CAP
NEPS = 1e-8
THRESHOLD = 0.9
KEY_ULP = 2.0 ** -24
FILLED = -6144.0
EMPTY = 8192.0
CF, NCF = {}, 0
for _name, _width in (("ident", P), ("sel", E), ("signA", 16), ("signB", 16), ("octet", NA), ("spare", S4), ("start", KT), ("need", KT),
                      ("step", ROUNDS * KT), ("offset", ROUNDS * KT)):
    CF[_name] = (NCF, NCF + _width)
    NCF += _width
CH, NCH = {}, 0
for _name, _width in (("tok", NT), ("iota", NA * NT), ("spread", P), ("ones", P), ("chunks", P), ("lower", P), ("levels", E * E)):
    CH[_name] = (NCH, NCH + _width)
    NCH += _width
QA, QB, QG = 13, 29, 45
NQ = QG + E * C4

SA = [[1, -1, -1, -1], [1, 1, -1, 1], [1, 1, 1, -1], [1, -1, 1, 1]]
SB = [[1, 1, 1, 1], [-1, 1, -1, 1], [-1, 1, 1, -1], [-1, -1, 1, 1]]


def build(nc, xt_d, x_d, small_d, w1_d, w2_d, cf_d, ch_d, out_d):
    probs_d = nc.dram_tensor("probs_scratch", (N * E, 1), FP32, kind="Internal").ap()
    ctx = ExitStack()
    with ctx:
        ctx.enter_context(nc.allow_low_precision(reason="counts up to 256 are exact in float16"))

        def sb(name, shape, dt=FP32):
            return ctx.enter_context(nc.sbuf_tensor(name, shape, dt))

        def sem(name):
            return ctx.enter_context(nc.semaphore(name))

        cf = sb("cf", [P, NCF])
        ch = sb("ch", [P, NCH], FP16)
        small = sb("small", [P, NQ])
        cfv = lambda k: cf[:, CF[k][0]:CF[k][1]]
        chv = lambda k: ch[:, CH[k][0]:CH[k][1]]

        sq = sb("sq", [P, 12])
        nrm = sb("nrm", [P, 12])
        facA = sb("facA", [P, 4, 4])
        facB = sb("facB", [P, 4, 4])
        ham = sb("ham", [P, 4, 4, 4])
        rot = sb("rot", [P, 4, 4])
        gprod = sb("gprod", [P, C4, E, C4])
        gfold = sb("gfold", [P, C4, GW])

        region = sb("region", [P, XRING * C4 * TG])
        xt = region[:, :].rearrange("p (r c n) -> p r c n", r=XRING, c=C4)
        lev = sb("lev", [P, NT, E, E], FP16)
        tk = lambda name: sb(name, [P, NT, E])
        cent, prob, rank, csum, arank, key = (tk(n) for n in ("cent", "prob", "rank", "csum", "arank", "key"))
        ulp = csum
        height = cent[:, :, :].bitcast(FP16)[:, :, 0:E]
        rmax = sb("rmax", [P, NT])
        rsum = sb("rsum", [P, NT])
        lowlev = sb("lowlev", [P, E, E])
        rstar = sb("rstar", [P, E])
        keys = sb("keys", [P, N // TC])
        hits = region[:, 0:KT * N // TC // 2].bitcast(FP16).rearrange("p (k n) -> p k n", k=KT)
        base = sb("base", [P, 2, KT])
        thr = sb("thr", [P, 2, KT])
        nxt = sb("nxt", [P, KT])
        cnt = sb("cnt", [P, 2, KT], FP16)
        passed = sb("passed", [P, KT])
        best = sb("best", [P, 1])
        tb = sb("tb", [P, E])
        mask = sb("mask", [P, E, 2, NT], FP16)
        seg = sb("seg", [P, E * 2 * NT], FP16)
        incl = sb("incl", [P, E, 2, NT], FP16)
        off = sb("off", [P, E, 2])
        places = region[:, N // 2:N].rearrange("p (q e t) -> p q e t", e=E, t=NT)
        pos = places[:, 0:2].rearrange("p q e t -> p (q e t)").rearrange("p (e m t) -> p e m t", m=2, t=NT)
        posi = places[:, 2].bitcast(I32)
        pab = places[:, 3:5].bitcast(I32).rearrange("p q e t -> p (q e t)").rearrange("p (e m t) -> p e m t", m=2, t=NT)
        ab = sb("ab", [P, E, 2, NT], FP16)
        hotA = sb("hotA", [P, NA, NT], FP16)
        hotB = sb("hotB", [P, 2 * NB, NT], FP16)
        tabU = sb("tabU", [2 * NB, NA], FP16)
        tabV = sb("tabV", [P, NA])
        tabf = sb("tabf", [P, S4])
        scat = sb("scat", [P, E, S4], U32)
        gath = sb("gath", [P, E, S4], U32)
        pidx = sb("pidx", [P, E, S4], U32)

        w1raw = sb("w1raw", [P, 2, C4, F])
        w2raw = sb("w2raw", [P, F4, D])
        w1rot = sb("w1rot", [P, C4, F])
        w1h = [sb(f"w1h{i}", [P, C4, F], F32R) for i in range(2)]
        w1l = [sb(f"w1l{i}", [P, C4, F], F32R) for i in range(2)]
        w2h = [sb(f"w2h{i}", [P, F4, D], F32R) for i in range(2)]
        w2l = [sb(f"w2l{i}", [P, F4, D], F32R) for i in range(2)]
        xg = sb("xg", [P, S4, D])
        xh = sb("xh", [P, C4, CAP], F32R)
        xl = sb("xl", [P, C4, CAP], F32R)
        hf = sb("hf", [P, 2, CAP])
        hh = sb("hh", [P, F4, CAP], F32R)
        hl = sb("hl", [P, F4, CAP], F32R)
        score = sb("score", [P, 2, S4])
        ysb = sb("ysb", [P, S4, D])
        warm = sb("warm", [P, 1])
        before = xg[:, 0:2, :].rearrange("p s d -> p (s d)").rearrange("p (t e f) -> p t e f", e=E, f=E)
        mass = xg[:, 2:4, :].rearrange("p s d -> p (s d)").rearrange("p (t e f) -> p t e f", e=E, f=E)
        parts = hf[:, :, 0:P]
        diag = ysb[:, :, :].rearrange("p s d -> p (s d)").rearrange("p (q c) -> p q c", c=P)

        bank = [ctx.enter_context(nc.psum_tensor(f"bank{i}", [P, 512], FP32)) for i in range(8)]
        xbank, hbank, ybank = bank[0:2], bank[2:4], bank[4:6]
        ubank, vbank = bank[6], bank[7]
        x0bank = lambda s: bank[(0, 1, 4, 5)[s]][:, :].rearrange("p (c n) -> p c n", c=C4)
        pbank, lbank, rbank = bank[1:3], [bank[i] for i in (0, 3, 5, 7)], bank[4]
        fbank, kbank, cbank, obank = [bank[i] for i in (6, 0, 3, 5)], bank[7], bank[1:3], (bank[3], bank[6])

        small_in, cf_in, ch_in = sem("small_in"), sem("cf_in"), sem("ch_in")
        xt_in = [sem(f"xt_in{i}") for i in range(XRING)]
        w1_in = [sem(f"w1_in{i}") for i in range(2)]
        w2_in = sem("w2_in")
        out_base, probs_out = sem("out_base"), sem("probs_out")
        squares, roots = sem("squares"), sem("roots")
        rot_ready, diag_ready, fold_mm = sem("rot_ready"), sem("diag_ready"), sem("fold_mm")
        gate_folded, parts_mm, parts_ev, logits_mm = sem("gate_folded"), sem("parts_mm"), sem("parts_ev"), sem("logits_mm")
        dve_step = sem("dve_step")
        centred, exped, prob_ready = sem("centred"), sem("exped"), sem("prob_ready")
        lev_ready, lev_mm = sem("lev_ready"), sem("lev_mm")
        key_ready, key_mm = sem("key_ready"), sem("key_mm")
        thr_ready, cnt_v, cnt_a, cnt_mm = sem("thr_ready"), sem("cnt_v"), sem("cnt_a"), sem("cnt_mm")
        base_ready, tb_mm = sem("base_ready"), sem("tb_mm")
        incl_ready, off_mm = sem("incl_ready"), sem("off_mm")
        hot_ready, u_mm, u_ev, v_mm, slots_ready = (sem(n) for n in ("hot_ready", "u_mm", "u_ev", "v_mm", "slots_ready"))
        xg_in = [sem(f"xg_in{i}") for i in range(S4)]
        score_in = [sem(f"score_in{i}") for i in range(2)]
        xt_mm, x_hi, x_lo = sem("xt_mm"), sem("x_hi"), sem("x_lo")
        w1_term, w1_rot, w1_hi, w1_lo = sem("w1_term"), sem("w1_rot"), sem("w1_hi"), sem("w1_lo")
        w2_hi, w2_lo = sem("w2_hi"), sem("w2_lo")
        h_mm, h_act, h_hi, h_lo = sem("h_mm"), sem("h_act"), sem("h_hi"), sem("h_lo")
        y_mm, y_ev = sem("y_mm"), sem("y_ev")
        added = [sem(f"added{i}") for i in range(S4)]

        block = ctx.enter_context(nc.Block())

        @block.sync
        def _(sp):
            sp.dma_start(small[:, :], small_d).then_inc(small_in, 16)

            def load_x(g):
                if g >= XRING:
                    sp.wait_ge(parts_mm, g - XRING + 1)
                sp.dma_start(xt[:, g % XRING], xt_d[g]).then_inc(xt_in[g % XRING], 16)

            def load_w1(e):
                if e >= 2:
                    sp.wait_ge(w1_rot, C4 * (e - 1))
                sp.dma_start(w1raw[:, e % 2], w1_d[e]).then_inc(w1_in[e % 2], 16)

            def load_w2(e):
                if e >= 1:
                    sp.wait_ge(w2_lo, e)
                if e == 1:
                    sp.wait_ge(xt_mm, S4)
                sp.dma_start(w2raw[:, :, :], w2_d[e]).then_inc(w2_in, 16)

            sp.dma_start(cf[:, :], cf_d).then_inc(cf_in, 16)
            load_x(0)
            load_x(1)
            sp.dma_start(ch[:, :], ch_d).then_inc(ch_in, 16)
            for g in range(2, NG):
                load_x(g)
            load_w1(0)
            load_w1(1)
            load_w2(0)
            sp.dma_start(out_d[0:N, :], x_d).then_inc(out_base, 16)
            sp.dma_start(out_d[N:N + SPARE, :], x_d[0:SPARE, :]).then_inc(out_base, 16)
            sp.wait_ge(prob_ready, len(CHUNKS))
            sp.dma_start(probs_d.rearrange("(p n) o -> p (n o)", p=P),
                         prob[:, :, :].rearrange("p t e -> p (t e)")).then_inc(probs_out, 16)
            for e in range(1, E):
                load_w2(e)
                if e + 1 < E:
                    load_w1(e + 1)
            for s in range(S4):
                sp.wait_ge(added[s], 16 * E)

        @block.gpsimd
        def _(pool):
            def gather_x(e):
                pool.wait_ge(slots_ready, e + 1)
                if e >= 1:
                    pool.wait_ge(xt_mm, C4 * e)
                for s in range(S4):
                    pool.indirect_dma_start(xg[:, s, :], None, x_d,
                                            bass.IndirectOffsetOnAxis(gath[:, e, s:s + 1], 0)).then_inc(xg_in[s], 16)

            def gather_scores(e):
                if e >= 2:
                    pool.wait_ge(y_ev, S4 * (e - 1))
                for s in range(S4):
                    pool.indirect_dma_start(score[:, e % 2, s:s + 1], None, probs_d,
                                            bass.IndirectOffsetOnAxis(pidx[:, e, s:s + 1], 0)).then_inc(score_in[e % 2], 16)

            def scatter(e, s):
                if e >= 1 and s == 0:
                    for k in range(S4):
                        pool.wait_ge(added[k], 16 * e)
                pool.wait_ge(y_ev, S4 * e + s + 1)
                pool.indirect_dma_start(out_d, bass.IndirectOffsetOnAxis(scat[:, e, s:s + 1], 0),
                                        ysb[:, s, :], None, compute_op=ALU.add).then_inc(added[s], 16)

            pool.wait_ge(probs_out, 16)
            gather_x(0)
            gather_scores(0)
            gather_x(1)
            gather_scores(1)
            pool.wait_ge(out_base, 32)
            for e in range(E):
                scatter(e, 0)
                scatter(e, 1)
                if e + 2 < E:
                    gather_x(e + 2)
                scatter(e, 2)
                scatter(e, 3)
                if e + 2 < E:
                    gather_scores(e + 2)

        @block.scalar
        def _(act):
            act.wait_ge(squares, 1)
            nc.scalar.activation(nrm[:, 4:6], nrm[:, 2:4], ACT.Sqrt).then_inc(roots, 1)

            def w1_first(e, j):
                if j == 0:
                    act.wait_ge(w1_in[e % 2], 16 * (e // 2 + 1))
                    act.wait_ge(w1_lo, C4 * e)
                nc.scalar.activation(w1rot[:, j, :], w1raw[:, e % 2, 0, :], ACT.Copy, scale=rot[:, j, 0:1]).then_inc(w1_term, 1)

            def w1_high(e, j):
                act.wait_ge(w1_rot, C4 * e + j + 1)
                if e >= 2:
                    act.wait_ge(h_mm, F4 * (e - 1))
                nc.scalar.activation(w1h[e % 2][:, j, :], w1rot[:, j, :], ACT.Copy).then_inc(w1_hi, 1)

            def w2_high(e):
                act.wait_ge(w2_in, 16 * (e + 1))
                if e >= 2:
                    act.wait_ge(y_mm, S4 * (e - 1))
                nc.scalar.activation(w2h[e % 2][:, :, :], w2raw[:, :, :], ACT.Copy).then_inc(w2_hi, 1)

            def x_high(e, j):
                act.wait_ge(xt_mm, C4 * e + j + 1)
                nc.scalar.activation(xh[:, j, :], xbank[j % 2][:, :], ACT.Copy).then_inc(x_hi, 1)

            def x_high0(s):
                act.wait_ge(xt_mm, s + 1)
                nc.scalar.activation(xh[:, :, s * P:(s + 1) * P], x0bank(s), ACT.Copy).then_inc(x_hi, 1)

            def hidden(e, f):
                n = F4 * e + f
                act.wait_ge(h_mm, n + 1)
                if n >= 2:
                    act.wait_ge(h_lo, n - 1)
                nc.scalar.activation(hf[:, n % 2, :], hbank[n % 2][:, :], ACT.Gelu).then_inc(h_act, 1)
                act.wait_ge(h_act, n + 1)
                if e >= 1:
                    act.wait_ge(y_mm, S4 * e)
                nc.scalar.activation(hh[:, f, :], hf[:, n % 2, :], ACT.Copy).then_inc(h_hi, 1)

            def y_out(e, s):
                n = S4 * e + s
                act.wait_ge(y_mm, n + 1)
                if s == 0:
                    act.wait_ge(score_in[e % 2], 16 * S4 * (e // 2 + 1))
                if e >= 1:
                    act.wait_ge(added[s], 16 * e)
                nc.scalar.activation(ysb[:, s, :], ybank[n % 2][:, :], ACT.Copy,
                                     scale=score[:, e % 2, s:s + 1]).then_inc(y_ev, 1)

            act.wait_ge(cf_in, 16)
            nc.scalar.activation(warm[:, :], cfv("ident")[:, 0:1], ACT.Exp)

            def diagonal(j):
                if j == 0:
                    act.wait_ge(rot_ready, 1)
                for i in range(C4):
                    last = nc.scalar.activation(diag[:, j * C4 + i, :], cfv("ident"), ACT.Copy, scale=rot[:, j, i:i + 1])
                last.then_inc(diag_ready, 1)

            def part_out(g):
                act.wait_ge(parts_mm, g + 1)
                if g >= 2:
                    act.wait_ge(logits_mm, g - 1)
                nc.scalar.activation(parts[:, g % 2, :], pbank[g % 2][:, 0:P], ACT.Copy).then_inc(parts_ev, 1)

            def exp(c):
                lo, hi = CHUNKS[c]
                act.wait_ge(centred, c + 1)
                nc.scalar.activation(cent[:, lo:hi], cent[:, lo:hi], ACT.Exp).then_inc(exped, 1)

            def w1_folded(j):
                act.wait_ge(fold_mm, j + 1)
                nc.scalar.activation(w1rot[:, j, :], fbank[j][:, :], ACT.Copy).then_inc(w1_rot, 1)

            g = 0
            for c, (_, hi) in enumerate(CHUNKS):
                while g < hi // TPG:
                    if g < C4:
                        diagonal(g)
                    part_out(g)
                    g += 1
                exp(c)
            w1_folded(0)
            w1_high(0, 0)
            for r in range(ROUNDS):
                act.wait_ge(thr_ready, r + 1)
                if r >= 2:
                    act.wait_ge(cnt_mm, r - 1)
                for k in range(KV, KT):
                    last = nc.scalar.activation(hits[:, k, :], keys[:, :], ACT.Sign, bias=thr[:, r % 2, k:k + 1],
                                                accum_out=cnt[:, r % 2, k:k + 1])
                last.then_inc(cnt_a, 1)
                if r == 1:
                    w1_folded(1)
                    w1_high(0, 1)
                if r == ROUNDS // 2 + 1:
                    w1_folded(2)
                    w1_high(0, 2)
            w1_folded(3)
            w1_high(0, 3)
            w2_high(0)
            nc.scalar.activation(warm[:, :], cfv("ident")[:, 0:1], ACT.Gelu)
            for s in range(S4):
                x_high0(s)
            w1_first(1, 0)
            for e in range(E):
                more = e + 1 < E
                hidden(e, 0)
                if more:
                    w1_first(e + 1, 1)
                hidden(e, 1)
                if more:
                    w1_high(e + 1, 0)
                hidden(e, 2)
                if more:
                    w1_high(e + 1, 1)
                    w1_first(e + 1, 2)
                hidden(e, 3)
                if more:
                    x_high(e + 1, 0)
                    x_high(e + 1, 1)
                    w1_first(e + 1, 3)
                    w1_high(e + 1, 2)
                y_out(e, 0)
                if more:
                    x_high(e + 1, 2)
                    x_high(e + 1, 3)
                    w1_high(e + 1, 3)
                y_out(e, 1)
                if more:
                    w2_high(e + 1)
                y_out(e, 2)
                if e + 2 < E:
                    w1_first(e + 2, 0)
                y_out(e, 3)

        @block.vector
        def _(dve):
            steps = [0]

            def then(ins):
                steps[0] += 1
                ins.then_inc(dve_step, 1)
                dve.wait_ge(dve_step, steps[0])

            def rotate_w1(e, j):
                dst = w1rot[:, j, :]
                dve.wait_ge(w1_term, C4 * (e - 1) + j + 1)
                for i in range(1, C4):
                    ins = nc.vector.scalar_tensor_tensor(dst, w1raw[:, e % 2, i, :], rot[:, j, i:i + 1], dst,
                                                         ALU.mult, ALU.add)
                    if i < C4 - 1:
                        then(ins)
                ins.then_inc(w1_rot, 1)

            def w1_low(e, j0, j1):
                dve.wait_ge(w1_hi, C4 * e + j1)
                nc.vector.tensor_tensor(w1l[e % 2][:, j0:j1, :], w1rot[:, j0:j1, :], w1h[e % 2][:, j0:j1, :].bitcast(FP32),
                                        ALU.subtract).then_inc(w1_lo, j1 - j0)

            def w2_low(e):
                dve.wait_ge(w2_hi, e + 1)
                nc.vector.tensor_tensor(w2l[e % 2][:, :, :], w2raw[:, :, :], w2h[e % 2][:, :, :].bitcast(FP32),
                                        ALU.subtract).then_inc(w2_lo, 1)

            def x_low(e, j):
                dve.wait_ge(x_hi, C4 * e + j + 1)
                nc.vector.tensor_tensor(xl[:, j, :], xbank[j % 2][:, :], xh[:, j, :].bitcast(FP32),
                                        ALU.subtract).then_inc(x_lo, 1)

            def x_low0(s):
                dve.wait_ge(x_hi, s + 1)
                nc.vector.tensor_tensor(xl[:, :, s * P:(s + 1) * P], x0bank(s), xh[:, :, s * P:(s + 1) * P].bitcast(FP32),
                                        ALU.subtract).then_inc(x_lo, 1)

            def h_low(e, f):
                n = F4 * e + f
                dve.wait_ge(h_hi, n + 1)
                nc.vector.tensor_tensor(hl[:, f, :], hf[:, n % 2, :], hh[:, f, :].bitcast(FP32),
                                        ALU.subtract).then_inc(h_lo, 1)

            def one_hots(e):
                if e >= 1:
                    dve.wait_ge(u_mm, e)
                iota = chv("iota").rearrange("p (a t) -> p a t", t=NT)
                nc.vector.tensor_tensor(hotA[:, :, :], ab[:, e, 0, :].unsqueeze(1).to_broadcast([P, NA, NT]),
                                        iota, ALU.is_equal)
                then(nc.vector.tensor_tensor(hotB[:, NB:, :], ab[:, e, 1, :].unsqueeze(1).to_broadcast([P, NB, NT]),
                                             iota[:, 0:NB, :], ALU.is_equal))
                nc.vector.tensor_tensor(hotB[:, 0:NB, :], hotB[:, NB:, :],
                                        chv("tok").unsqueeze(1).to_broadcast([P, NB, NT]), ALU.mult).then_inc(hot_ready, 1)

            def table_rows(e):
                dve.wait_ge(u_mm, e + 1)
                nc.vector.tensor_copy(tabU[:, :], ubank[0:2 * NB, 0:NA]).then_inc(u_ev, 1)

            def slot_tables(e):
                dve.wait_ge(v_mm, e + 1)
                then(nc.vector.tensor_tensor(tabV[:, :], vbank[:, 0:NA], cfv("octet"), ALU.mult))
                then(nc.vector.tensor_reduce(tabf[:, :], tabV[:, :].rearrange("p (g c) -> p c g", c=S4), AX.X, ALU.add))
                nc.vector.scalar_tensor_tensor(scat[:, e, :], tabf[:, :], EMPTY, cfv("spare"), ALU.add, ALU.min)
                then(nc.vector.tensor_scalar(tabV[:, 0:S4], tabf[:, :], EMPTY, float(N - 1), ALU.add, ALU.min))
                nc.vector.tensor_scalar(pidx[:, e, :], tabV[:, 0:S4], float(E), float(e), ALU.mult, ALU.add)
                nc.vector.tensor_copy(gath[:, e, :], tabV[:, 0:S4]).then_inc(slots_ready, 1)

            def count_tokens(e0, e1):
                w = e1 - e0
                flat = lambda x: x[:, e0:e1].rearrange("p e m t -> p (e m t)")
                for m, op in enumerate((ALU.is_gt, ALU.is_equal)):
                    ins = nc.vector.tensor_tensor(mask[:, e0:e1, m, :].rearrange("p e t -> p t e"), key[:, :, e0:e1],
                                                  tb[:, e0:e1].unsqueeze(1).to_broadcast([P, NT, w]), op)
                then(ins)
                nc.vector.tensor_tensor_scan(flat(incl), seg[:, 0:w * 2 * NT], flat(mask), 0.0, ALU.mult,
                                             ALU.add).then_inc(incl_ready, 1)

            def places(e0, e1):
                w = e1 - e0
                flat = lambda x: x[:, e0:e1].rearrange("p e m t -> p (e m t)")
                dve.wait_ge(off_mm, 1 if e0 == 0 else 2)
                counts = obank[0 if e0 == 0 else 1]
                low = counts[:, 0:2 * w].rearrange("p (e m) -> p e m", m=2)
                tot = counts[:, 2 * w:4 * w].rearrange("p (e m) -> p e m", m=2)
                then(nc.vector.tensor_scalar(off[:, e0:e1, :], low, 1.0 + 2 * N, None, ALU.subtract))
                then(nc.vector.tensor_tensor(off[:, e0:e1, 1:2], off[:, e0:e1, 1:2], tot[:, :, 0:1], ALU.add))
                then(nc.vector.tensor_tensor(pos[:, e0:e1], incl[:, e0:e1],
                                             off[:, e0:e1, :].unsqueeze(3).to_broadcast([P, w, 2, NT]), ALU.add))
                then(nc.vector.tensor_tensor(flat(pos), flat(pos), flat(mask), ALU.mult))
                then(nc.vector.scalar_tensor_tensor(posi[:, e0:e1], pos[:, e0:e1, 0, :], 2.0 * N, pos[:, e0:e1, 1, :],
                                                    ALU.add, ALU.add))
                nc.vector.tensor_scalar(pab[:, e0:e1, 0, :], posi[:, e0:e1], 4, None, ALU.logical_shift_right)
                then(nc.vector.tensor_scalar(pab[:, e0:e1, 1, :], posi[:, e0:e1], NB - 1, None, ALU.bitwise_and))
                then(nc.vector.tensor_copy(flat(ab), flat(pab)))

            nc.vector.memset(gfold[:, :, :], 0.0)
            dve.wait_ge(small_in, 16)
            then(nc.vector.tensor_tensor(sq[:, :], small[:, 0:12], small[:, 0:12], ALU.mult))
            nc.vector.tensor_reduce(nrm[:, 0:1], sq[:, 0:8], AX.X, ALU.add)
            then(nc.vector.tensor_reduce(nrm[:, 1:2], sq[:, 8:12], AX.X, ALU.add))
            nc.vector.tensor_scalar(nrm[:, 2:4], nrm[:, 0:2], NEPS, None, ALU.add).then_inc(squares, 1)
            dve.wait_ge(cf_in, 16)
            nc.vector.tensor_tensor(facA[:, :, :].rearrange("p i k -> p (i k)"), small[:, QA:QB], cfv("signA"), ALU.mult)
            then(nc.vector.tensor_tensor(facB[:, :, :].rearrange("p j k -> p (j k)"), small[:, QB:QG], cfv("signB"), ALU.mult))
            then(nc.vector.tensor_tensor(ham[:, :, :, :], facA[:, :, :].unsqueeze(1).to_broadcast([P, 4, 4, 4]),
                                         facB[:, :, :].unsqueeze(2).to_broadcast([P, 4, 4, 4]), ALU.mult))
            nc.vector.tensor_reduce(rot[:, :, :], ham[:, :, :, :], AX.X, ALU.add)
            dve.wait_ge(roots, 1)
            then(nc.vector.reciprocal(nrm[:, 6:8], nrm[:, 4:6]))
            then(nc.vector.tensor_tensor(nrm[:, 6:8], nrm[:, 6:8], nrm[:, 2:4], ALU.mult))
            then(nc.vector.tensor_tensor(nrm[:, 6:8], nrm[:, 6:8], nrm[:, 4:6], ALU.add))
            then(nc.vector.tensor_tensor(nrm[:, 8:9], nrm[:, 6:7], nrm[:, 7:8], ALU.mult))
            then(nc.vector.reciprocal(nrm[:, 9:10], nrm[:, 8:9]))
            then(nc.vector.tensor_scalar(nrm[:, 10:11], nrm[:, 9:10], small[:, 12:13], 4.0, ALU.mult, ALU.mult))
            nc.vector.tensor_scalar(rot[:, :, :], rot[:, :, :], nrm[:, 10:11], None, ALU.mult).then_inc(rot_ready, 1)
            dve.wait_ge(rot_ready, 1)
            gw = small[:, QG:NQ].rearrange("p (e c) -> p e c", c=C4)
            then(nc.vector.tensor_tensor(gprod[:, :, :, :], rot[:, :, :].unsqueeze(2).to_broadcast([P, C4, E, C4]),
                                         gw.unsqueeze(1).to_broadcast([P, C4, E, C4]), ALU.mult))
            nc.vector.tensor_reduce(gfold[:, :, 0:E], gprod[:, :, :, :], AX.X, ALU.add).then_inc(gate_folded, 1)
            nc.vector.memset(seg[:, :], 1.0)
            then(nc.vector.memset(before, 0.0))
            nc.vector.memset(seg[:, :].rearrange("p (g t) -> p g t", t=NT)[:, :, 0:1], 0.0)

            def route(c):
                lo, hi = CHUNKS[c]
                w = hi - lo
                sl = slice(lo, hi)
                logits = lbank[c][:, 0:w * GW].rearrange("p (t x) -> p t x", x=GW)[:, :, 0:E]
                bef, mas = before[:, 0:w], mass[:, 0:w]
                wide = lambda a: a.unsqueeze(2).to_broadcast([P, w, E])
                dve.wait_ge(logits_mm, hi // TPG)
                then(nc.vector.tensor_reduce(rmax[:, sl], logits, AX.X, ALU.max))
                nc.vector.tensor_tensor(cent[:, sl], logits, wide(rmax[:, sl]), ALU.subtract).then_inc(centred, 1)
                dve.wait_ge(exped, c + 1)
                then(nc.vector.tensor_reduce(rsum[:, sl], cent[:, sl], AX.X, ALU.add))
                then(nc.vector.reciprocal(rsum[:, sl], rsum[:, sl]))
                nc.vector.tensor_tensor(prob[:, sl], cent[:, sl], wide(rsum[:, sl]), ALU.mult).then_inc(prob_ready, 1)
                dve.wait_ge(prob_ready, c + 1)
                for e in range(E):
                    for f0, f1, op in ((0, e, ALU.is_ge), (e + 1, E, ALU.is_gt)):
                        if f0 < f1:
                            last = nc.vector.tensor_tensor(bef[:, :, e, f0:f1], prob[:, sl, f0:f1],
                                                           prob[:, sl, e:e + 1].to_broadcast([P, w, f1 - f0]), op)
                then(last)
                nc.vector.tensor_reduce(rank[:, sl], bef, AX.X, ALU.add)
                then(nc.vector.tensor_tensor(mas, bef, prob[:, sl].unsqueeze(2).to_broadcast([P, w, E, E]), ALU.mult))
                nc.vector.tensor_reduce(csum[:, sl], mas, AX.X, ALU.add)
                then(nc.vector.tensor_scalar(arank[:, sl], rank[:, sl], -1.0, float(E + 1), ALU.mult, ALU.add))
                nc.vector.scalar_tensor_tensor(height[:, sl], csum[:, sl], THRESHOLD, arank[:, sl], ALU.is_lt, ALU.mult)
                then(nc.vector.scalar_tensor_tensor(key[:, sl], rank[:, sl], 1.0, prob[:, sl], ALU.add, ALU.subtract))
                if c == 0:
                    dve.wait_ge(ch_in, 16)
                nc.vector.tensor_tensor(lev[:, sl], height[:, sl].unsqueeze(2).to_broadcast([P, w, E, E]),
                                        chv("levels").rearrange("p (r e) -> p r e", e=E).unsqueeze(1).to_broadcast([P, w, E, E]),
                                        ALU.is_ge).then_inc(lev_ready, 1)
                nc.vector.tensor_scalar(ulp[:, sl], rank[:, sl], 0.0, KEY_ULP, ALU.is_equal, ALU.mult)
                then(nc.vector.scalar_tensor_tensor(key[:, sl], rank[:, sl], 1.0, key[:, sl], ALU.add, ALU.subtract))
                nc.vector.scalar_tensor_tensor(key[:, sl], key[:, sl], KEY_MID, ulp[:, sl], ALU.subtract, ALU.subtract)

            for c in range(len(CHUNKS)):
                route(c)
            dve.wait_ge(lev_mm, 1)
            then(nc.vector.tensor_scalar(lowlev[:, :, :], rbank[:, 0:E * E].rearrange("p (r e) -> p e r", e=E),
                                         float(CAP), None, ALU.is_lt))
            then(nc.vector.tensor_reduce(rstar[:, :], lowlev[:, :, :], AX.X, ALU.add))
            then(nc.vector.scalar_tensor_tensor(arank[:, :, :], rstar[:, :].unsqueeze(1).to_broadcast([P, NT, E]), float(E + 1),
                                                height[:, :, :], ALU.subtract, ALU.add))
            then(nc.vector.scalar_tensor_tensor(key[:, :, :], arank[:, :, :], 4.0, key[:, :, :], ALU.mult, ALU.add))
            nc.vector.tensor_scalar(key[:, :, :], key[:, :, :], 2.0, -1.0, ALU.min, ALU.max).then_inc(key_ready, 1)
            table = lambda k, r: cfv(k)[:, r * KT:(r + 1) * KT]
            nc.vector.tensor_copy(base[:, 0, :], cfv("start"))
            w1_low(0, 0, 1)
            dve.wait_ge(key_mm, 1)
            nc.vector.tensor_copy(keys[:, :], kbank[:, 0:N // TC])
            nc.vector.tensor_tensor(thr[:, 0, :], cfv("start"), table("offset", 0), ALU.add).then_inc(thr_ready, 1)
            dve.wait_ge(thr_ready, 1)

            for r in range(ROUNDS):
                now, new = r % 2, (r + 1) % 2
                if r >= 2:
                    dve.wait_ge(cnt_mm, r - 1)
                for k in range(KV):
                    last = nc.vector.tensor_scalar(hits[:, k, :], keys[:, :], thr[:, now, k:k + 1], None, ALU.is_ge, ALU.add,
                                                   accum_out=cnt[:, now, k:k + 1])
                last.then_inc(cnt_v, 1)
                if r >= 1:
                    then(nc.vector.scalar_tensor_tensor(base[:, now, :], table("step", r - 1), best[:, :], base[:, new, :],
                                                        ALU.mult, ALU.add))
                if r + 1 < ROUNDS:
                    nc.vector.tensor_tensor(nxt[:, :], base[:, now, :], table("offset", r + 1), ALU.add)
                dve.wait_ge(cnt_mm, r + 1)
                then(nc.vector.scalar_tensor_tensor(passed[:, :], cbank[now][:, 0:KT], 0.0, cfv("need"), ALU.add,
                                                    ALU.is_ge, accum_out=best[:, :]))
                if r + 1 < ROUNDS:
                    nc.vector.scalar_tensor_tensor(thr[:, new, :], table("step", r), best[:, :], nxt[:, :], ALU.mult,
                                                   ALU.add).then_inc(thr_ready, 1)
                    dve.wait_ge(thr_ready, r + 2)
                else:
                    nc.vector.scalar_tensor_tensor(base[:, new, :], table("step", r), best[:, :], base[:, now, :],
                                                   ALU.mult, ALU.add).then_inc(base_ready, 1)

            w1_low(0, 1, 2)
            dve.wait_ge(tb_mm, 1)
            then(nc.vector.tensor_copy(tb[:, :], kbank[:, 0:E]))
            count_tokens(0, 2)
            places(0, 2)
            one_hots(0)
            w1_low(0, 2, C4)
            table_rows(0)
            slot_tables(0)
            one_hots(1)
            w2_low(0)
            table_rows(1)
            count_tokens(2, E)
            x_low0(0)
            slot_tables(1)
            for s in range(1, S4):
                x_low0(s)
            places(2, E)

            for e in range(E):
                more, later = e + 1 < E, e + 2 < E
                if e >= 1:
                    w2_low(e)
                if more:
                    rotate_w1(e + 1, 0)
                h_low(e, 0)
                if more:
                    rotate_w1(e + 1, 1)
                h_low(e, 1)
                if later:
                    one_hots(e + 2)
                h_low(e, 2)
                if more:
                    rotate_w1(e + 1, 2)
                h_low(e, 3)
                if more:
                    x_low(e + 1, 0)
                    x_low(e + 1, 1)
                if later:
                    table_rows(e + 2)
                if more:
                    rotate_w1(e + 1, 3)
                    x_low(e + 1, 2)
                    x_low(e + 1, 3)
                if later:
                    slot_tables(e + 2)
                if more:
                    w1_low(e + 1, 0, C4)

        @block.tensor
        def _(pe):
            ident = cfv("ident")

            def slot_rows(e):
                pe.wait_ge(hot_ready, e + 1)
                if e >= 1:
                    pe.wait_ge(u_ev, e)
                for t in range(NT):
                    last = nc.tensor.matmul(ubank[0:2 * NB, 0:NA], hotB[:, :, t], hotA[:, :, t],
                                            start=(t == 0), stop=(t == NT - 1))
                last.then_inc(u_mm, 1)

            def slot_spread(e):
                pe.wait_ge(u_ev, e + 1)
                if e >= 1:
                    pe.wait_ge(slots_ready, e)
                nc.tensor.matmul(vbank[:, 0:NA], chv("spread")[0:2 * NB, :], tabU[:, :],
                                 start=True, stop=True).then_inc(v_mm, 1)

            def transpose_x(e, chunks):
                for s in range(S4):
                    pe.wait_ge(xg_in[s], 16 * (e + 1))
                for j in chunks:
                    if e >= 1 and C4 * e + j >= C4 + 2:
                        pe.wait_ge(x_lo, C4 * e + j - 1)
                    elif e == 1:
                        pe.wait_ge(x_lo, C4)
                    for s in range(S4):
                        last = nc.tensor.transpose(xbank[j % 2][:, s * P:(s + 1) * P], xg[:, s, j * P:(j + 1) * P], ident)
                    last.then_inc(xt_mm, 1)

            def transpose_x0():
                for s in range(S4):
                    pe.wait_ge(xg_in[s], 16)
                    for j in range(C4):
                        last = nc.tensor.transpose(x0bank(s)[:, j, :], xg[:, s, j * P:(j + 1) * P], ident)
                    last.then_inc(xt_mm, 1)
                    if s == S4 - 2:
                        keep_clock(2)

            def keep_clock(n):
                for _ in range(n):
                    nc.tensor.matmul(cbank[1][:, :], chv("ones"), ch[:, 0:512], start=True, stop=True)

            def split_product(dst, ah, al, bh, bl, first, last):
                nc.tensor.matmul(dst, ah, bh, start=first, stop=False)
                nc.tensor.matmul(dst, ah, bl, start=False, stop=False)
                return nc.tensor.matmul(dst, al, bh, start=False, stop=last)

            def layer1(e, f):
                if f == 0:
                    pe.wait_ge(w1_lo, C4 * (e + 1))
                    if e == 0:
                        pe.wait_ge(x_lo, S4)
                n = F4 * e + f
                if n >= 2:
                    pe.wait_ge(h_act, n - 1)
                fs = slice(f * P, (f + 1) * P)
                for j in range(C4):
                    if f == 0 and e >= 1:
                        pe.wait_ge(x_lo, C4 * e + j + 1)
                    last = split_product(hbank[n % 2][:, :], w1h[e % 2][:, j, fs], w1l[e % 2][:, j, fs],
                                         xh[:, j, :], xl[:, j, :], j == 0, j == C4 - 1)
                last.then_inc(h_mm, 1)

            def layer2(e, s):
                if s == 0:
                    pe.wait_ge(w2_lo, e + 1)
                n = S4 * e + s
                if n >= 2:
                    pe.wait_ge(y_ev, n - 1)
                ss = slice(s * P, (s + 1) * P)
                for f in range(F4):
                    if s == 0:
                        pe.wait_ge(h_lo, F4 * e + f + 1)
                    last = split_product(ybank[n % 2][:, :], hh[:, f, ss], hl[:, f, ss],
                                         w2h[e % 2][:, f, :], w2l[e % 2][:, f, :], f == 0, f == F4 - 1)
                last.then_inc(y_mm, 1)

            def gate(g):
                pe.wait_ge(xt_in[g % XRING], 16 * (g // XRING + 1))
                if g >= 2:
                    pe.wait_ge(parts_ev, g - 1)
                for j in range(C4):
                    for u in range(TPG):
                        last = nc.tensor.matmul(pbank[g % 2][u * GW:(u + 1) * GW, 0:P], gfold[:, j, :],
                                                xt[:, g % XRING, j, u * P:(u + 1) * P], start=(j == 0), stop=(j == C4 - 1))
                last.then_inc(parts_mm, 1)

            def logits_by_token(g):
                pe.wait_ge(parts_ev, g + 1)
                c = next(c for c, (lo, hi) in enumerate(CHUNKS) if lo <= g * TPG < hi)
                at = g * TPG * GW - CHUNKS[c][0] * GW
                nc.tensor.transpose(lbank[c][:, at:at + P], parts[:, g % 2, :], ident).then_inc(logits_mm, 1)

            def count_ranks(c):
                pe.wait_ge(lev_ready, c + 1)
                for t in range(*CHUNKS[c]):
                    last = nc.tensor.matmul(rbank[:, 0:E * E], chv("ones"), lev[:, t].rearrange("p r e -> p (r e)"),
                                            start=(t == 0), stop=(t == NT - 1))
                if c == len(CHUNKS) - 1:
                    last.then_inc(lev_mm, 1)

            def fold(j, i):
                term = nc.tensor.matmul(fbank[j][:, :], diag[:, j * C4 + i, :], w1raw[:, 0, i, :],
                                        start=(i == 0), stop=(i == C4 - 1))
                if i == C4 - 1:
                    term.then_inc(fold_mm, 1)

            pe.wait_ge(gate_folded, 1)
            for g in range(NG):
                gate(g)
                if g == 0:
                    pe.wait_ge(cf_in, 16)
                logits_by_token(g)
            pe.wait_ge(ch_in, 16)
            count_ranks(0)
            count_ranks(1)
            pe.wait_ge(diag_ready, C4)
            pe.wait_ge(w1_in[0], 16)
            for i in range(C4):
                fold(0, i)
            count_ranks(2)
            count_ranks(3)
            fold(1, 0)
            fold(1, 1)
            pe.wait_ge(centred, len(CHUNKS))
            pe.wait_ge(cf_in, 16)
            pe.wait_ge(key_ready, 1)
            for c in range(NT // TC):
                last = nc.tensor.transpose(kbank[:, c * P:(c + 1) * P],
                                           key[:, c * TC:(c + 1) * TC, :].rearrange("p t e -> p (t e)"), ident)
            last.then_inc(key_mm, 1)
            fold(1, 2)
            fold(1, 3)
            for r in range(ROUNDS):
                fold(2 + r // C4, r % C4)
                pe.wait_ge(cnt_v, r + 1)
                pe.wait_ge(cnt_a, r + 1)
                nc.tensor.matmul(cbank[r % 2][:, 0:KT], chv("chunks"), cnt[:, r % 2, :],
                                 start=True, stop=True).then_inc(cnt_mm, 1)
            pe.wait_ge(base_ready, 1)
            nc.tensor.matmul(kbank[:, 0:E], base[:, ROUNDS % 2, 0:1].to_broadcast([P, P]), cfv("sel"),
                             start=True, stop=True).then_inc(tb_mm, 1)

            def count_before(n, e0, e1):
                pe.wait_ge(incl_ready, n + 1)
                ends = incl[:, e0:e1, :, NT - 1].rearrange("p e m -> p (e m)")
                w = 2 * (e1 - e0)
                nc.tensor.matmul(obank[n][:, 0:w], chv("lower"), ends, start=True, stop=True)
                nc.tensor.matmul(obank[n][:, w:2 * w], chv("ones"), ends, start=True, stop=True).then_inc(off_mm, 1)

            pe.wait_ge(w1_rot, C4)
            count_before(0, 0, 2)
            slot_rows(0)
            slot_spread(0)
            keep_clock(4)
            slot_rows(1)
            keep_clock(3)
            slot_spread(1)
            transpose_x0()
            count_before(1, 2, E)
            keep_clock(7)
            for e in range(E):
                for f in range(F4):
                    layer1(e, f)
                if e + 1 < E:
                    transpose_x(e + 1, (0, 1))
                if e + 2 < E:
                    slot_rows(e + 2)
                layer2(e, 0)
                if e + 1 < E:
                    transpose_x(e + 1, (2, 3))
                if e + 2 < E:
                    slot_spread(e + 2)
                for s in range(1, S4):
                    layer2(e, s)


def shape_constants():
    p = np.arange(P)
    cf = np.zeros((P, NCF), np.float32)
    ch = np.zeros((P, NCH), np.float16)
    cf[:, slice(*CF["ident"])] = np.eye(P)
    cf[:, slice(*CF["sel"])] = p[:, None] == np.arange(E)[None]
    cf[:, slice(*CF["signA"])] = np.ravel(SA)[None]
    cf[:, slice(*CF["signB"])] = np.ravel(np.transpose(SB))[None]
    k = np.arange(KT)
    act = k >= KV
    sign = np.where(act, -1.0, 1.0)
    cf[:, slice(*CF["start"])] = -KEY_MID * sign
    cf[:, slice(*CF["need"])] = np.where(act, 2.0 * CAP - N, CAP)
    for r in range(ROUNDS):
        step = float(KT + 1) ** -(r + 1)
        cf[:, CF["step"][0] + r * KT:CF["step"][0] + (r + 1) * KT] = sign * step
        cf[:, CF["offset"][0] + r * KT:CF["offset"][0] + (r + 1) * KT] = sign * ((k + 1) * step - act * KEY_ULP / 2)
    cf[:, slice(*CF["octet"])] = np.arange(NA)[None] // S4 == p[:, None] % (P // NB)
    cf[:, slice(*CF["spare"])] = N + p[:, None] * S4 + np.arange(S4)[None]
    ch[:, slice(*CH["tok"])] = np.arange(NT)[None] + p[:, None] * NT - N // 2
    ch[:, slice(*CH["iota"])] = np.repeat(np.arange(NA), NT)[None]
    b_of_p = p // (P // NB)
    spread = np.zeros((P, P))
    for b in range(NB):
        spread[b] = b_of_p == b
        spread[NB + b] = (b_of_p == b) * FILLED
    ch[:, slice(*CH["spread"])] = spread
    ch[:, slice(*CH["ones"])] = 1
    ch[:, slice(*CH["chunks"])] = p[:, None] % E == p[None] % E
    ch[:, slice(*CH["lower"])] = p[:, None] < p[None]
    ch[:, slice(*CH["levels"])] = np.repeat(E + 2 - np.arange(1, E + 1), E)[None]
    return cf, ch


def kernel(x, cond_256, L0_cond_q_right, L0_cond_spectral_gate, L0_ffn_gate_w, L0_ffn_w1, L0_ffn_w2):
    import concourse.bacc as bacc
    from concourse.bass_utils import run_bass_kernel_spmd

    rows = np.ascontiguousarray(np.asarray(x).reshape(N, D))
    xt = np.ascontiguousarray(rows.reshape(P, NG, TPG, C4, P).transpose(1, 4, 3, 2, 0)).reshape(NG, P, C4, TG)
    cond, right = np.asarray(cond_256).T, np.asarray(L0_cond_q_right).T
    xor = np.arange(4)[:, None] ^ np.arange(4)[None]
    gw = np.asarray(L0_ffn_gate_w).reshape(E, C4, P).transpose(2, 0, 1).reshape(P, E * C4)
    small = np.ascontiguousarray(np.concatenate(
        [cond, right, np.asarray(L0_cond_spectral_gate).reshape(P, 1), cond[:, xor.ravel()], right[:, xor.ravel()], gw], axis=1))
    w1 = np.ascontiguousarray(np.asarray(L0_ffn_w1).reshape(E, F, C4, P).transpose(0, 3, 2, 1))
    w2 = np.ascontiguousarray(np.asarray(L0_ffn_w2).reshape(E, D, F4, P).transpose(0, 3, 2, 1))
    cf, ch = shape_constants()

    nc = bacc.Bacc("TRN2", target_bir_lowering=False, num_devices=1)
    arrays, aps = {}, []
    for name, a in (("xt", xt), ("x", rows), ("small", small), ("w1", w1), ("w2", w2), ("cf", cf), ("ch", ch)):
        arrays[f"in_{name}"] = a
        aps.append(nc.dram_tensor(f"in_{name}", a.shape, mybir.dt.from_np(a.dtype), kind="ExternalInput").ap())
    out = nc.dram_tensor("out", (N + SPARE, D), FP32, kind="ExternalOutput").ap()
    build(nc, *aps, out)
    r = run_bass_kernel_spmd(nc, [arrays], core_ids=[0])
    return np.asarray(r.results[0]["out"])[0:N].reshape(B, T_SEQ, D)
```
